# Optimizing a Trainium2 kernel written in Bass

```python
import numpy as np
import jax
import jax.numpy as jnp

def _softmax(x, axis=-1):
    return jax.nn.softmax(x, axis=axis)

def _gelu(x):
    return jax.nn.gelu(x, approximate=True)

def _silu(x):
    return jax.nn.silu(x)

def _sigmoid(x):
    return jax.nn.sigmoid(x)

def _layernorm(x, axis=-1, eps=1e-05):
    m = jnp.mean(x, axis=axis, keepdims=True)
    v = jnp.var(x, axis=axis, keepdims=True)
    return (x - m) / jnp.sqrt(v + eps)

def _scatter_add(tgt, idx, src, axis=0):
    return tgt.at[idx].add(src)

def _segment_sum(src, seg, n):
    return jax.ops.segment_sum(src, seg, n)
kernel_name = 'mk_sandwich_d1_jaxref_r8_477394'

def setup_inputs(seed: int=0):
    np.random.seed(seed)
    _w = jnp.asarray

    def _L0_attn_setup():
        import jax, jax.numpy as jnp
        import numpy as np
        import math
        D = 256
        NH = 16
        HD = D // NH

        def rotary_apply(x, cos, sin):
            d = x.shape[-1]
            x1, x2 = (x[..., :d // 2], x[..., d // 2:])
            c, s = (cos[..., :d // 2], sin[..., :d // 2])
            return jnp.concatenate([x1 * c - x2 * s, x2 * c + x1 * s], axis=-1)
        key = jax.random.key(seed)
        k1, k2, k3 = jax.random.split(key, 3)
        x = jax.random.normal(k1, (2, 256, D), dtype=jnp.float32)
        w_qkv = jax.random.normal(k2, (D, 3 * D), dtype=jnp.float32) * (1.0 / math.sqrt(D))
        w_o = jax.random.normal(k3, (D, D), dtype=jnp.float32) * (1.0 / math.sqrt(D))
        return {'x': x, 'w_qkv': w_qkv, 'w_o': w_o}
    _L0_attn_in = _L0_attn_setup()

    def _L0_ffn_setup():
        import jax, jax.numpy as jnp
        import numpy as np
        import math
        B, S, D = (2, 128, 256)
        H, KVH, HD = (16, 4, 128)
        E, K, FF = (8, 2, 896)
        EPS = 1e-05
        ROPE_BASE = 1000000.0

        def rmsnorm(x, w, eps=EPS):
            xf = x.astype(jnp.float32)
            var = jnp.mean(xf * xf, axis=-1, keepdims=True)
            return (xf * jax.lax.rsqrt(var + eps)).astype(x.dtype) * w

        def apply_rope(x, cos, sin):
            x1 = x[..., 0::2]
            x2 = x[..., 1::2]
            r1 = x1 * cos - x2 * sin
            r2 = x1 * sin + x2 * cos
            return jnp.stack([r1, r2], axis=-1).reshape(x.shape)
        key = jax.random.key(seed)
        ks = jax.random.split(key, 12)
        sc = 0.02
        inp = {'x': jax.random.normal(ks[0], (B, S, D), jnp.float32), 'ln_w': jnp.ones((D,), jnp.float32), 'ff_ln_w': jnp.ones((D,), jnp.float32), 'wq': jax.random.normal(ks[1], (D, H * HD), jnp.float32) * sc, 'wk': jax.random.normal(ks[2], (D, KVH * HD), jnp.float32) * sc, 'wv': jax.random.normal(ks[3], (D, KVH * HD), jnp.float32) * sc, 'wo': jax.random.normal(ks[4], (H * HD, D), jnp.float32) * sc, 'gate_w': jax.random.normal(ks[5], (D, E), jnp.float32) * sc, 'w1': jax.random.normal(ks[6], (E, D, FF), jnp.float32) * sc, 'w3': jax.random.normal(ks[7], (E, D, FF), jnp.float32) * sc, 'w2': jax.random.normal(ks[8], (E, FF, D), jnp.float32) * sc}
        return inp
    _L0_ffn_in = _L0_ffn_setup()
    _d = {'L0_attn_x': _L0_attn_in['x'], 'L0_attn_w_qkv': _L0_attn_in['w_qkv'], 'L0_attn_w_o': _L0_attn_in['w_o'], 'L0_ffn_ln_w': _L0_ffn_in['ln_w'], 'L0_ffn_ff_ln_w': _L0_ffn_in['ff_ln_w'], 'L0_ffn_wq': _L0_ffn_in['wq'], 'L0_ffn_wk': _L0_ffn_in['wk'], 'L0_ffn_wv': _L0_ffn_in['wv'], 'L0_ffn_wo': _L0_ffn_in['wo'], 'L0_ffn_gate_w': _L0_ffn_in['gate_w'], 'L0_ffn_w1': _L0_ffn_in['w1'], 'L0_ffn_w3': _L0_ffn_in['w3'], 'L0_ffn_w2': _L0_ffn_in['w2']}
    _x0 = _d['L0_attn_x']
    _d['L0_attn_x'] = jax.random.normal(jax.random.fold_in(jax.random.key(seed), 1), (1, 2048, 256), dtype=_x0.dtype)
    del _x0
    return _d

def reference(L0_attn_x, L0_attn_w_qkv, L0_attn_w_o, L0_ffn_ln_w, L0_ffn_ff_ln_w, L0_ffn_wq, L0_ffn_wk, L0_ffn_wv, L0_ffn_wo, L0_ffn_gate_w, L0_ffn_w1, L0_ffn_w3, L0_ffn_w2):

    def _L0_attn_ref(x, w_qkv, w_o):
        import jax, jax.numpy as jnp
        import numpy as np
        import math
        D = 256
        NH = 16
        HD = D // NH

        def rotary_apply(x, cos, sin):
            d = x.shape[-1]
            x1, x2 = (x[..., :d // 2], x[..., d // 2:])
            c, s = (cos[..., :d // 2], sin[..., :d // 2])
            return jnp.concatenate([x1 * c - x2 * s, x2 * c + x1 * s], axis=-1)
        B, T, _ = x.shape
        qkv = (x @ w_qkv).reshape(B, T, 3, NH, HD)
        q, k, v = (qkv[:, :, 0], qkv[:, :, 1], qkv[:, :, 2])
        inv_freq = 1.0 / 10000.0 ** (jnp.arange(0, HD, 2, dtype=jnp.float32) / HD)
        t = jnp.arange(T, dtype=jnp.float32)
        freqs = jnp.outer(t, inv_freq)
        emb = jnp.concatenate([freqs, freqs], axis=-1)
        cos = jnp.cos(emb)[None, None]
        sin = jnp.sin(emb)[None, None]
        q = rotary_apply(jnp.transpose(q, (0, 2, 1, 3)), cos, sin)
        k = rotary_apply(jnp.transpose(k, (0, 2, 1, 3)), cos, sin)
        v = jnp.transpose(v, (0, 2, 1, 3))
        scores = jnp.einsum('bhqd,bhkd->bhqk', q, k) / math.sqrt(HD)
        causal = jnp.tril(jnp.ones((T, T), dtype=bool))
        scores = jnp.where(causal, scores, -jnp.inf)
        attn = jax.nn.softmax(scores, axis=-1)
        out = jnp.einsum('bhqk,bhkd->bhqd', attn, v)
        out = jnp.transpose(out, (0, 2, 1, 3)).reshape(B, T, D)
        return out @ w_o

    def _L0_ffn_ref(x, ln_w, ff_ln_w, wq, wk, wv, wo, gate_w, w1, w3, w2):
        import jax, jax.numpy as jnp
        import numpy as np
        import math
        B, S, D = (2, 128, 256)
        H, KVH, HD = (16, 4, 128)
        E, K, FF = (8, 2, 896)
        EPS = 1e-05
        ROPE_BASE = 1000000.0

        def rmsnorm(x, w, eps=EPS):
            xf = x.astype(jnp.float32)
            var = jnp.mean(xf * xf, axis=-1, keepdims=True)
            return (xf * jax.lax.rsqrt(var + eps)).astype(x.dtype) * w

        def apply_rope(x, cos, sin):
            x1 = x[..., 0::2]
            x2 = x[..., 1::2]
            r1 = x1 * cos - x2 * sin
            r2 = x1 * sin + x2 * cos
            return jnp.stack([r1, r2], axis=-1).reshape(x.shape)
        Bx, Sx, Dx = x.shape
        residual = x
        h = rmsnorm(x, ln_w)
        q = (h @ wq).reshape(Bx, Sx, H, HD)
        k = (h @ wk).reshape(Bx, Sx, KVH, HD)
        v = (h @ wv).reshape(Bx, Sx, KVH, HD)
        pos = jnp.arange(Sx, dtype=jnp.float32)
        inv_freq = ROPE_BASE ** (-jnp.arange(0, HD, 2, dtype=jnp.float32) / HD)
        ang = pos[:, None] * inv_freq[None, :]
        cos = jnp.cos(ang)[None, :, None, :]
        sin = jnp.sin(ang)[None, :, None, :]
        q = apply_rope(q, cos, sin)
        k = apply_rope(k, cos, sin)
        rep = H // KVH
        k = jnp.repeat(k, rep, axis=2)
        v = jnp.repeat(v, rep, axis=2)
        scores = jnp.einsum('bqhd,bkhd->bhqk', q, k) / math.sqrt(HD)
        causal = jnp.tril(jnp.ones((Sx, Sx), dtype=bool))
        scores = jnp.where(causal[None, None], scores, jnp.finfo(scores.dtype).min)
        attn = jax.nn.softmax(scores, axis=-1)
        o = jnp.einsum('bhqk,bkhd->bqhd', attn, v).reshape(Bx, Sx, H * HD)
        x = o @ wo + residual
        residual = x
        h = rmsnorm(x, ff_ln_w)
        ht = h.reshape(-1, Dx)
        logits = ht @ gate_w
        top_vals, top_idx = jax.lax.top_k(logits, K)
        gates = jax.nn.softmax(top_vals, axis=-1)
        out = jnp.zeros_like(ht)
        for e in range(E):
            we = jnp.sum(gates * (top_idx == e), axis=-1)
            ye = jax.nn.silu(ht @ w1[e]) * (ht @ w3[e]) @ w2[e]
            out = out + we[:, None] * ye
        return out.reshape(Bx, Sx, Dx) + residual
    x = L0_attn_x
    x = x + _layernorm(_L0_attn_ref(_layernorm(x, axis=-1), L0_attn_w_qkv, L0_attn_w_o), axis=-1)
    x = x + _layernorm(_L0_ffn_ref(_layernorm(x, axis=-1), L0_ffn_ln_w, L0_ffn_ff_ln_w, L0_ffn_wq, L0_ffn_wk, L0_ffn_wv, L0_ffn_wo, L0_ffn_gate_w, L0_ffn_w1, L0_ffn_w3, L0_ffn_w2), axis=-1)
    return x

_drawn_inputs = setup_inputs


def setup_inputs(seed=0):
    import zlib

    import numpy as np

    out = dict(_drawn_inputs(seed))
    spreads = {'L0_ffn_ln_w': (1.0, 0.6), 'L0_ffn_ff_ln_w': (1.0, 0.6)}
    factors = {'L0_ffn_wq': 8.0,
     'L0_ffn_wk': 8.0,
     'L0_ffn_gate_w': 6.519,
     'L0_ffn_w1': 5.856,
     'L0_ffn_w3': 5.813,
     'L0_ffn_w2': 5.801}
    for name, (base, spread) in spreads.items():
        noise = np.random.default_rng([zlib.crc32(name.encode()), seed]).standard_normal(out[name].shape)
        drawn = base * np.exp(spread * noise) if base else spread * noise
        out[name] = jnp.asarray(drawn.astype(out[name].dtype))
    for name, factor in factors.items():
        out[name] = (out[name] * factor).astype(out[name].dtype)
    return out
```

```python
from contextlib import ExitStack

import concourse.bass as bass
import numpy as np
from concourse import mybir

F32 = mybir.dt.float32
F32R = mybir.dt.float32r
BF16 = mybir.dt.bfloat16
ALU = mybir.AluOpType
ACT = mybir.ActivationFunctionType
AX = mybir.AxisListType

P = 128
T = 2048
D = 256
DK = D // P
NT = T // P
CH = 512
NC = T // CH
TPC = CH // P
EPS = 1e-5
NEG = -1e38

HA, HDA = 16, 16
SCALE_A = 1.0 / float(np.sqrt(HDA))
HPT = P // HDA
UA = 2 * D // P
HB, KVB, HDB = 16, 4, 128
SCALE_B = 1.0 / float(np.sqrt(HDB))
REP = HB // KVB
NE, TOPK, FF = 8, 2, 896
FT = FF // P

QUADS = [(i, q) for i in range(NC) for q in range(i + 1)]
PAIRS = 2 * len(QUADS)
PIECES = [(i, c, min(CH, (i + 1) * P - c * CH)) for i in range(NT) for c in range(i // TPC + 1)]



def wait_apart(eng, sem, value, passed):
    eng.wait_ge(sem, value + 1)
    eng.sem_inc(passed, 1)


class Chain:

    def __init__(self, eng, sem, passed, base=0):
        self.eng, self.sem, self.passed, self.base, self.n = eng, sem, passed, base, 0

    def link(self, ins):
        ins.then_inc(self.sem, 1)
        self.n += 1
        wait_apart(self.eng, self.sem, self.base + self.n, self.passed)


class Core:

    def __init__(self, nc, root):
        self.nc, self.root = nc, root
        self.closed = []
        self.passed = self.sem("passed")

    def sem(self, name):
        self.closed.append(self.root.enter_context(self.nc.semaphore(name)))
        return self.closed[-1]

    def open_semaphores(self, eng):
        for s in self.closed:
            eng.sem_inc(s, 1)
        self.closed = []

    def keep(self, name, shape, dt=F32):
        return self.root.enter_context(self.nc.sbuf_tensor(name, shape, dt))

    def scratch(self, name, shape, dt=F32):
        return self.nc.dram_tensor(name, shape, dt, kind="Internal").ap()


def phase_sbuf(nc, stack):
    def sb(name, shape, dt=F32):
        return stack.enter_context(nc.sbuf_tensor(name, shape, dt))
    return sb


def raw(ap):
    return ap.bitcast(F32)


def three_products(nc, out, w_hi, w_lo, x_hi, x_lo, first, last):
    nc.tensor.matmul(out, w_hi, x_hi, start=first, stop=False, skip_group_check=True)
    nc.tensor.matmul(out, w_lo, x_hi, start=False, stop=False, skip_group_check=True)
    return nc.tensor.matmul(out, w_hi, x_lo, start=False, stop=last, skip_group_check=True)



def root(core, act, out, var, asked, asked_at, answered):
    act.wait_ge(asked, asked_at + 1)
    core.nc.scalar.activation(out, var, ACT.Sqrt, bias=core.eps[:]).then_inc(answered, 1)


def layer_norm_stats(nc, chain, core, src, answered, answer):
    for t in range(TPC):
        last = nc.vector.bn_stats(core.stats[:, t, :], src(t))
    chain.link(last)
    for t in range(TPC):
        last = nc.vector.bn_aggr(core.mv[:, t, :], core.stats[:, t, :])
    chain.link(last)
    chain.eng.wait_ge(answered, answer + 1)
    chain.link(nc.vector.reciprocal(core.rstd[:], core.rstd[:]))


def rms_norm_stats(nc, chain, core, src, answered, answer):
    for t in range(TPC):
        last = nc.vector.bn_stats(core.stats[:, t, :], src(t))
    chain.link(last)
    for t in range(TPC):
        last = nc.vector.bn_aggr(core.mv[:, t, :], core.stats[:, t, :])
    chain.link(last)
    chain.link(nc.vector.tensor_tensor(core.rstd[:, :, :], core.mv[:, :, 0:1], core.mv[:, :, 0:1], ALU.mult))
    chain.link(nc.vector.tensor_tensor(core.rstd[:, :, :], core.rstd[:, :, :], core.mv[:, :, 1:2], ALU.add))
    chain.eng.wait_ge(answered, answer + 1)
    chain.link(nc.vector.reciprocal(core.rstd[:], core.rstd[:]))


def phase_norm(core, tag, mode, hT, gate=None, load=None):
    nc = core.nc
    hT_hi, hT_lo = hT
    which = {"ln": 0, "ln_rms": 1, "rms": 2}[mode]
    with ExitStack() as st:
        sb = phase_sbuf(nc, st)
        xn = sb(f"xn_{tag}", [P, TPC, D])
        hf = sb(f"hf_{tag}", [P, DK, CH])
        tr = st.enter_context(nc.psum_tensor(f"tr_{tag}", [P, DK, CH], F32))
        pl = st.enter_context(nc.psum_tensor(f"pl_{tag}", [P, CH], F32))
        loaded = core.sem(f"loaded_{tag}")
        normed = core.sem(f"normed_{tag}")
        transposed = core.sem(f"transposed_{tag}")
        hi_done = core.sem(f"hi_done_{tag}")
        lo_done = core.sem(f"lo_done_{tag}")
        chained = core.sem(f"chained_{tag}")
        hf_done = core.sem(f"hf_done_{tag}")
        routed = core.sem(f"routed_{tag}")
        rooted = core.sem(f"rooted_{tag}")
        logits_out = core.sem(f"logits_out_{tag}")
        with nc.Block() as block:
            @block.sync
            def _(sp):
                core.open_semaphores(sp)
                if load:
                    load(sp, loaded)

            n_loads = load.count if load else 0
            CHAIN = {"ln": 4, "ln_rms": 10, "rms": 6}[mode]
            ROOTS = {"ln": 1, "ln_rms": 2, "rms": 1}[mode]

            @block.vector
            def _(dve):
                if load:
                    dve.wait_ge(loaded, 16 * n_loads + 1)
                    nc.vector.memset(core.ones[:], 1.0)
                    nc.vector.memset(core.eps[:], EPS)
                with dve.Fori(0, NC) as c:
                    chain = Chain(dve, chained, core.passed, c * CHAIN)
                    src = core.R if mode == "rms" else core.X
                    tile = lambda t: src[:, bass.ds(c * TPC + t, 1), :].rearrange("p a d -> p (a d)")
                    if mode != "rms":
                        layer_norm_stats(nc, chain, core, tile, rooted, c * ROOTS + 1)
                    dve.wait_ge(transposed, c + 1)
                    if mode == "ln":
                        for t in range(TPC):
                            last = nc.vector.tensor_scalar(xn[:, t, :], tile(t), core.mv[:, t, 0:1],
                                                           core.rstd[:, t, :], ALU.subtract, ALU.mult)
                        chain.link(last)
                        last_done = None
                    else:
                        if mode == "ln_rms":
                            for t in range(TPC):
                                rt = core.R[:, bass.ds(c * TPC + t, 1), :].rearrange("p a d -> p (a d)")
                                last = nc.vector.tensor_scalar(rt, tile(t), core.mv[:, t, 0:1],
                                                               core.rstd[:, t, :], ALU.subtract, ALU.mult)
                            chain.link(last)
                        rtile = lambda t: core.R[:, bass.ds(c * TPC + t, 1), :].rearrange("p a d -> p (a d)")
                        rms_norm_stats(nc, chain, core, rtile, rooted, (c + 1) * ROOTS)
                        for t in range(TPC):
                            last = nc.vector.tensor_scalar(xn[:, t, :], rtile(t), core.rstd[:, t, :], None, ALU.mult)
                        chain.link(last)
                    assert chain.n == CHAIN, chain.n
                    for dk in range(DK):
                        dve.wait_ge(hi_done, c * DK + dk + 2)
                        lo = nc.vector.scalar_tensor_tensor(
                            hT_lo[:, dk, bass.ds(c * CH, CH)], tr[:, dk, :], core.wcol[:, which, dk:dk + 1],
                            hT_hi[:, dk, bass.ds(c * CH, CH)], ALU.mult, ALU.subtract)
                        lo.then_inc(lo_done, 1)
                    if gate is not None:
                        dve.wait_ge(routed, c + 2)
                        nc.vector.tensor_copy(
                            core.logits[:, bass.ds(c * TPC, TPC), :],
                            pl[:, 0:TPC * NE].rearrange("p (t e) -> p t e", e=NE)).then_inc(logits_out, 1)

            @block.tensor
            def _(pe):
                with pe.Fori(0, NC) as c:
                    pe.wait_ge(chained, (c + 1) * CHAIN + 1)
                    pe.wait_ge(lo_done, c * DK + 1)
                    if gate is not None:
                        pe.wait_ge(hf_done, c * DK + 1)
                    for dk in range(DK):
                        for t in range(TPC):
                            last = nc.tensor.transpose(tr[:, dk, t * P:(t + 1) * P],
                                                       xn[:, t, dk * P:(dk + 1) * P], core.ident[:])
                    last.then_inc(transposed, 1)
                    if gate is not None:
                        pe.wait_ge(hf_done, (c + 1) * DK + 1)
                        pe.wait_ge(logits_out, c + 1)
                        for t in range(TPC):
                            for dk in range(DK):
                                last = nc.tensor.matmul(pl[:, t * NE:(t + 1) * NE], hf[:, dk, t * P:(t + 1) * P],
                                                        gate[:, dk, :], start=(dk == 0), stop=(dk == DK - 1))
                        last.then_inc(routed, 1)

            @block.scalar
            def _(act):
                with act.Fori(0, NC) as c:
                    if mode != "rms":
                        root(core, act, core.rstd[:], core.mv[:, :, 1:2], chained, c * CHAIN + 2, rooted)
                    if mode != "ln":
                        root(core, act, core.rstd[:], core.rstd[:], chained, (c + 1) * CHAIN - 2, rooted)
                    act.wait_ge(transposed, c + 2)
                    for dk in range(DK):
                        nc.scalar.activation(hT_hi[:, dk, bass.ds(c * CH, CH)], tr[:, dk, :], ACT.Copy,
                                             scale=core.wcol[:, which, dk:dk + 1]).then_inc(hi_done, 1)
                    if gate is not None:
                        act.wait_ge(routed, c + 1)
                        for dk in range(DK):
                            act.wait_ge(lo_done, c * DK + dk + 2)
                            nc.scalar.activation(hf[:, dk, :], tr[:, dk, :], ACT.Copy,
                                                 scale=core.wcol[:, which, dk:dk + 1]).then_inc(hf_done, 1)


def phase_project_a(core, hT, V_all, wa_in, cos_in, sin_in):
    nc = core.nc
    hT_hi, hT_lo = hT
    NQK, NW = 2 * D, 5 * D
    with ExitStack() as st:
        sb = phase_sbuf(nc, st)
        w_raw = sb("wa_raw", [P, DK, NW])
        w_hi = sb("wa_hi", [P, DK, NW], F32R)
        w_lo = sb("wa_lo", [P, DK, NW], F32R)
        cos = sb("cos_a", [P, T])
        sin = sb("sin_a", [P, T])
        rot = sb("rot_a", [P, 3, CH])
        r_hi = sb("r_hi_a", [P, 2, CH], F32R)
        r_lo = sb("r_lo_a", [P, 2, CH], F32R)
        ps = st.enter_context(nc.psum_tensor("ps_pa", [P, 2, 2, CH], F32))
        pv = st.enter_context(nc.psum_tensor("pv_pa", [P, 2, CH], F32))
        w_loaded, w_split, w_high = core.sem("wa_loaded"), core.sem("wa_split"), core.sem("wa_high")
        projected, rotated, chained = core.sem("pa_projected"), core.sem("pa_rotated"), core.sem("pa_chained")
        hi_done, lo_done = core.sem("pa_hi"), core.sem("pa_lo")
        stored = [core.sem(f"pa_stored{i}") for i in range(2)]
        v_done, v_out = core.sem("pa_v_done"), core.sem("pa_v_out")
        UNITS = UA * NC
        with nc.Block() as block:
            @block.sync
            def _(sp):
                core.open_semaphores(sp)
                sp.dma_start(w_raw[:], wa_in).then_inc(w_loaded, 16)
                sp.dma_start(cos[:], cos_in).then_inc(w_loaded, 16)
                sp.dma_start(sin[:], sin_in).then_inc(w_loaded, 16)
                with sp.Fori(0, NC) as c:
                    for u in range(UA):
                        for part, buf, done in ((0, r_hi, hi_done), (1, r_lo, lo_done)):
                            sp.wait_ge(done, c * UA + u + 2)
                            dst = core.qk_a[u * HPT:(u + 1) * HPT, part, :, bass.ds(c * CH, CH)]
                            sp.dma_start(dst, raw(buf[:, u % 2, :])).then_inc(stored[u % 2], 16)
                for i in range(2):
                    sp.wait_ge(stored[i], UNITS // 2 * 32 + 1)

            @block.tensor
            def _(pe):
                pe.wait_ge(w_split, 2)
                with pe.Fori(0, NC) as c:
                    for u in range(UA):
                        if u >= 2:
                            pe.wait_ge(rotated, c * UA + u)
                        else:
                            pe.wait_ge(rotated, c * UA + 1)
                        for swap in range(2):
                            o = u * P + swap * 3 * D
                            for dk in range(DK):
                                last = three_products(
                                    nc, ps[:, u % 2, swap, :], w_hi[:, dk, o:o + P], w_lo[:, dk, o:o + P],
                                    hT_hi[:, dk, bass.ds(c * CH, CH)], hT_lo[:, dk, bass.ds(c * CH, CH)],
                                    dk == 0, dk == DK - 1)
                        last.then_inc(projected, 1)
                for t in range(NT):
                    if t >= 2:
                        pe.wait_ge(v_out, t)
                    for dk in range(DK):
                        last = three_products(nc, pv[:, t % 2, 0:D],
                                              hT_hi[:, dk, t * P:(t + 1) * P], hT_lo[:, dk, t * P:(t + 1) * P],
                                              w_hi[:, dk, NQK:NQK + D], w_lo[:, dk, NQK:NQK + D],
                                              dk == 0, dk == DK - 1)
                    last.then_inc(v_done, 1)

            @block.vector
            def _(dve):
                dve.wait_ge(w_high, 2)
                nc.vector.tensor_tensor(w_lo[:], w_raw[:], w_hi[:], ALU.subtract).then_inc(w_split, 1)
                with dve.Fori(0, NC) as c:
                    chain = Chain(dve, chained, core.passed, c * UA)
                    for u in range(UA):
                        dve.wait_ge(projected, c * UA + u + 2)
                        dve.wait_ge(hi_done, c * UA + u + 1)
                        nc.vector.tensor_tensor(rot[:, 0, :], ps[:, u % 2, 0, :], cos[:, bass.ds(c * CH, CH)], ALU.mult)
                        chain.link(nc.vector.tensor_tensor(rot[:, 1, :], ps[:, u % 2, 1, :],
                                                           sin[:, bass.ds(c * CH, CH)], ALU.mult))
                        nc.vector.tensor_tensor(rot[:, 2, :], rot[:, 0, :], rot[:, 1, :], ALU.add).then_inc(rotated, 1)
                        dve.wait_ge(hi_done, c * UA + u + 2)
                        nc.vector.tensor_tensor(r_lo[:, u % 2, :], rot[:, 2, :], r_hi[:, u % 2, :],
                                                ALU.subtract).then_inc(lo_done, 1)

            @block.scalar
            def _(act):
                act.wait_ge(w_loaded, 49)
                nc.scalar.activation(w_hi[:], w_raw[:], ACT.Copy).then_inc(w_high, 1)
                with act.Fori(0, NC) as c:
                    for u in range(UA):
                        act.wait_ge(rotated, c * UA + u + 2)
                        if u >= 2:
                            act.wait_ge(stored[u % 2], c * (UA // 2 * 32) + 32 + 1)
                        else:
                            act.wait_ge(stored[u % 2], c * (UA // 2 * 32) + 1)
                        nc.scalar.activation(r_hi[:, u % 2, :], rot[:, 2, :], ACT.Copy).then_inc(hi_done, 1)
                for t in range(NT):
                    act.wait_ge(v_done, t + 2)
                    nc.scalar.activation(V_all[:, t, :], pv[:, t % 2, 0:D], ACT.Copy).then_inc(v_out, 1)


def phase_attention_a(core, V_all, O_all):
    nc = core.nc
    SR = 4 * HDA
    VW = 32
    NB = 3
    SLOW = len(QUADS) - 2
    PPQ = len(PIECES) // SLOW
    assert PPQ * SLOW == len(PIECES)
    NQ, NPC = len(QUADS), len(PIECES)
    ends = {QUADS.index((i, i)): i for i in range(NC)}
    with ExitStack() as st:
        sb = phase_sbuf(nc, st)
        Q = [sb(f"Qst{i}", [P, T], F32R) for i in range(NB)]
        K = [sb(f"Kst{i}", [P, T], F32R) for i in range(NB)]
        V = [sb(f"Vh{i}", [P, NT, VW]) for i in range(NB)]
        p = sb("p_a", [P, 4, 2, CH])
        oT = sb("oT_a", [P, CH])
        mxp = sb("mxp_a", [P, NT, NC])
        nm = sb("nm_a", [P, NT])
        nmT_hi = sb("nmT_hi_a", [NT, P], F32R)
        nmT_lo = sb("nmT_lo_a", [NT, P], F32R)
        osum = sb("osum_a", [P, TPC, HDA + 1])
        orec = sb("orec_a", [P, TPC, 1])
        ps = st.enter_context(nc.psum_tensor("ps_aa", [P, 2, 2, CH], F32))
        pm = st.enter_context(nc.psum_tensor("pm_aa", [P, 2, CH], F32))
        po = st.enter_context(nc.psum_tensor("po_aa", [P, CH], F32))
        pt = st.enter_context(nc.psum_tensor("pt_aa", [P, CH], F32))
        qk_loaded = [core.sem(f"aa_qk_loaded{i}") for i in range(NB)]
        max_loaded = [core.sem(f"aa_max_loaded{i}") for i in range(NB)]
        k_padded, q_padded, v_ready = core.sem("aa_k_padded"), core.sem("aa_q_padded"), core.sem("aa_v_ready")
        v_padded, m_padded = core.sem("aa_v_padded"), core.sem("aa_m_padded")
        piece_done, piece_max, max_ready = core.sem("aa_piece_done"), core.sem("aa_piece_max"), core.sem("aa_max_ready")
        max_T, max_hi, max_lo = core.sem("aa_max_T"), core.sem("aa_max_hi"), core.sem("aa_max_lo")
        scored, exped, valued = core.sem("aa_scored"), core.sem("aa_exped"), core.sem("aa_valued")
        o_copied, o_T, o_summed, o_done = core.sem("aa_o_copied"), core.sem("aa_o_T"), core.sem("aa_o_summed"), core.sem("aa_o_done")
        chained = core.sem("aa_chained")

        def steps(eng, step, peel=0):
            def three(j):
                step((NB * j, 0, j), (NB * j + 1, 1, j))
                step((NB * j + 1, 1, j), (NB * j + 2, 2, j))
                step((NB * j + 2, 2, j), (NB * j + 3, 0, j + 1))
            step(None, (0, 0, 0))
            turns = (HA - 1) // NB
            with eng.Fori(0, turns - peel) as j:
                three(j)
            if peel:
                three(turns - 1)
            step((HA - 1, 0, turns), None)
        assert (HA - 1) % NB == 0

        def wait(eng, s, value):
            if not isinstance(value, int) or value > 0:
                eng.wait_ge(s, value + 1)

        with nc.Block() as block:
            @block.sync
            def _(sp):
                core.open_semaphores(sp)
                def load(head, par):
                    wait(sp, scored, (head - 2) * PAIRS)
                    for part in range(2):
                        src = core.qk_a[bass.ds(head, 1), part, :, :].rearrange("a r t -> (a r) t")
                        for rep in range(2):
                            r0 = (2 * part + rep) * HDA
                            sp.dma_start(raw(Q[par][r0:r0 + HDA, :]), src).then_inc(qk_loaded[par], 16)
                        src = core.qk_a[bass.ds(head + HA, 1), part, :, :].rearrange("a r t -> (a r) t")
                        for rep in range(2):
                            r0 = (2 * rep + part) * HDA
                            sp.dma_start(raw(K[par][r0:r0 + HDA, :]), src).then_inc(qk_loaded[par], 16)

                def step(t, m):
                    if m is not None:
                        h, par, use = m
                        if t is not None and not (isinstance(h, int) and h == HA - 1):
                            load(h + 1, (par + 1) % NB)
                        sp.wait_ge(max_hi, h + 2)
                        sp.dma_start(raw(Q[par][SR:SR + 1, :]), raw(nmT_hi[:])).then_inc(max_loaded[par], 16)
                        sp.wait_ge(max_lo, h + 2)
                        sp.dma_start(raw(Q[par][SR + 1:SR + 2, :]), raw(nmT_lo[:])).then_inc(max_loaded[par], 16)
                load(0, 0)
                load(1, 1)
                steps(sp, step, peel=1)

            @block.gpsimd
            def _(pool):
                def step(t, m):
                    if m is not None:
                        h, par, use = m
                        if not isinstance(h, int):
                            before = NB * use if par == 2 else h - 2 if par == 0 else NB * use
                            wait_apart(pool, valued, before * NQ, core.passed)
                        nc.gpsimd.memset(raw(Q[par][SR:SR + 2, :]), 0.0).then_inc(q_padded, 1)
                        pool.wait_ge(q_padded, h + 2)
                        src = V_all[:, :, bass.ds(h * HDA, HDA)]
                        nc.gpsimd.tensor_copy(V[par][:, :, 0:HDA], src).then_inc(v_ready, 1)
                        pool.wait_ge(v_ready, h + 2)
                pool.wait_ge(k_padded, 3 * NB + 1)
                pool.wait_ge(v_padded, 2 * NB + 1)
                steps(pool, step)

            @block.tensor
            def _(pe):
                pe.wait_ge(k_padded, 3 * NB + 1)

                def step(t, m):
                    if t is not None:
                        th, tp, tu = t
                    if m is not None:
                        mh, mp, mu = m
                        pe.wait_ge(qk_loaded[mp], (mu + 1) * 128 + 1)
                        pe.wait_ge(q_padded, mh + 2)
                        wait(pe, max_lo, mh)

                    def piece(k):
                        i, c, w = PIECES[k]
                        wait(pe, piece_max, mh * NPC + k - 1)
                        diag = c == i // TPC
                        out = pm[:, k % 2, 0:w]
                        last = nc.tensor.matmul(out, Q[mp][:, i * P:(i + 1) * P], K[mp][:, c * CH:c * CH + w],
                                                start=True, stop=not diag, skip_group_check=True)
                        if diag:
                            last = nc.tensor.matmul(pm[:, k % 2, w - P:w], core.identb[:], core.maskq[:],
                                                    start=False, stop=True, skip_group_check=True)
                        last.then_inc(piece_done, 1)

                    def scores(n, half):
                        i, q = QUADS[n]
                        pair = 2 * n + half
                        pe.wait_ge(exped, th * PAIRS + max(0, pair - 1) + 1)
                        for j in range(2):
                            g = 2 * half + j
                            kt = TPC * q + g
                            out = ps[:, half, j, :]
                            last = nc.tensor.matmul(out, K[tp][:, kt * P:(kt + 1) * P], Q[tp][:, i * CH:(i + 1) * CH],
                                                    start=True, stop=q < i, skip_group_check=True)
                            if q == i:
                                w = (g + 1) * P
                                last = nc.tensor.matmul(ps[:, half, j, 0:w], core.identb[:],
                                                        core.maskt[:, 3 * P - g * P:3 * P - g * P + w],
                                                        start=False, stop=True, skip_group_check=True)
                        last.then_inc(scored, 1)

                    def values(n):
                        i, q = QUADS[n]
                        pe.wait_ge(exped, th * PAIRS + 2 * n + 2 + 1)
                        if q == 0:
                            wait(pe, o_copied, th * NC + i)
                        for g in range(TPC):
                            pair = 2 * n + g // 2
                            last = nc.tensor.matmul(po[g * VW:(g + 1) * VW, :], V[tp][:, TPC * q + g, :],
                                                    p[:, pair % 4, g % 2, :], start=(q == 0), stop=(q == i),
                                                    skip_group_check=True)
                        last.then_inc(valued, 1)

                    def turn(i):
                        pe.wait_ge(o_copied, th * NC + i + 2)
                        wait(pe, o_summed, th * NC + i)
                        for r in range(TPC):
                            last = nc.tensor.transpose(pt[:, r * P:(r + 1) * P], oT[:, r * P:(r + 1) * P], core.ident[:])
                        last.then_inc(o_T, 1)

                    if t is not None:
                        pe.wait_ge(max_loaded[tp], (tu + 1) * 32 + 1)
                        pe.wait_ge(v_ready, th + 2)
                    k = 0
                    for n in range(NQ):
                        for half in range(2):
                            if t is not None:
                                scores(n, half)
                            if m is not None and n < SLOW:
                                for _ in range(2):
                                    piece(k)
                                    k += 1
                        if t is not None and n >= 1:
                            values(n - 1)
                        if m is not None and n < SLOW:
                            piece(k)
                            k += 1
                        if t is not None and n - 2 in ends:
                            turn(ends[n - 2])
                        if m is not None and n == SLOW:
                            pe.wait_ge(max_ready, mh + 2)
                            nc.tensor.transpose(pm[0:NT, 0, 0:P], nm[:, :], core.ident[:]).then_inc(max_T, 1)
                    if t is not None:
                        values(NQ - 1)
                        turn(NC - 1)
                steps(pe, step)

            @block.scalar
            def _(act):
                def step(t, m):
                    def copy_out(i):
                        act.wait_ge(valued, (t[0] * NQ + [n for n in ends if ends[n] == i][0] + 1) + 1)
                        wait(act, o_T, t[0] * NC + i)
                        nc.scalar.activation(oT[:], po[:], ACT.Copy).then_inc(o_copied, 1)

                    for n in range(NQ):
                        if t is not None:
                            th = t[0]
                            for half in range(2):
                                pair = 2 * n + half
                                act.wait_ge(scored, th * PAIRS + pair + 2)
                                wait(act, valued, th * NQ + n - 1 if n >= 1 else th * NQ)
                                nc.scalar.activation(p[:, pair % 4, :, :], ps[:, half, :, :], ACT.Exp,
                                                     scale=SCALE_A).then_inc(exped, 1)
                            if n - 1 in ends:
                                copy_out(ends[n - 1])
                        if m is not None and n == SLOW:
                            act.wait_ge(max_T, m[0] + 2)
                            prev, uses = (m[1] - 1) % NB, m[2] + (m[1] > 0)
                            wait(act, max_loaded[prev], uses * 32)
                            nc.scalar.activation(nmT_hi[:], pm[0:NT, 0, 0:P], ACT.Copy).then_inc(max_hi, 1)
                    if t is not None:
                        copy_out(NC - 1)
                steps(act, step)

            @block.vector
            def _(dve):
                for i in range(NB):
                    nc.vector.memset(raw(K[i][SR:P, :]), 0.0).then_inc(k_padded, 1)
                    nc.vector.memset(raw(Q[i][SR:P, :]), 0.0).then_inc(k_padded, 1)
                    nc.vector.memset(V[i][:], 0.0).then_inc(v_padded, 1)
                nc.vector.memset(mxp[:], 3e38).then_inc(m_padded, 1)
                dve.wait_ge(m_padded, 2)
                dve.wait_ge(k_padded, 2 * NB + 1)
                dve.wait_ge(v_padded, NB + 1)
                for i in range(NB):
                    nc.vector.memset(raw(K[i][SR:SR + 2, :]), 1.0).then_inc(k_padded, 1)
                    nc.vector.memset(V[i][:, :, HDA:HDA + 1], 1.0).then_inc(v_padded, 1)

                def step(t, m):
                    def finish(i):
                        th = t[0]
                        dve.wait_ge(o_T, th * NC + i + 2)
                        wait(dve, o_done, th * NC + i)
                        src = pt[:, :].rearrange("p (t g v) -> p t v g", t=TPC, v=VW)[:, :, 0:HDA + 1, :]
                        nc.vector.tensor_reduce(osum[:], src, axis=AX.X, op=ALU.add).then_inc(o_summed, 1)
                        dve.wait_ge(o_summed, th * NC + i + 2)
                        nc.vector.reciprocal(orec[:], osum[:, :, HDA:HDA + 1]).then_inc(chained, 1)
                        dve.wait_ge(chained, th * NC + i + 2)
                        nc.vector.tensor_tensor(O_all[:, i * TPC:(i + 1) * TPC, bass.ds(th * HDA, HDA)],
                                                osum[:, :, 0:HDA], orec[:].broadcast_to([P, TPC, HDA]),
                                                ALU.mult).then_inc(o_done, 1)

                    k = 0
                    for n in range(NQ):
                        if m is not None and n < SLOW:
                            for _ in range(PPQ):
                                i, c, w = PIECES[k]
                                dve.wait_ge(piece_done, m[0] * NPC + k + 2)
                                nc.vector.tensor_reduce(mxp[:, i, c:c + 1], pm[:, k % 2, 0:w], axis=AX.X,
                                                        op=ALU.max, negate=True).then_inc(piece_max, 1)
                                k += 1
                        if m is not None and n == SLOW - 1:
                            dve.wait_ge(piece_max, (m[0] + 1) * NPC + 1)
                            nc.vector.tensor_reduce(nm[:], mxp[:], axis=AX.X, op=ALU.min).then_inc(max_ready, 1)
                        if t is not None and n - 2 in ends:
                            finish(ends[n - 2])
                        if m is not None and n == SLOW:
                            dve.wait_ge(max_hi, m[0] + 2)
                            nc.vector.tensor_tensor(nmT_lo[:], pm[0:NT, 0, 0:P], nmT_hi[:],
                                                    ALU.subtract).then_inc(max_lo, 1)
                    if t is not None:
                        finish(NC - 1)
                steps(dve, step)


def phase_output_a(core, O_all, woa_in):
    nc = core.nc
    with ExitStack() as st:
        sb = phase_sbuf(nc, st)
        wo = sb("woa", [P, DK, D])
        wo_hi = sb("woa_hi", [P, DK, D], F32R)
        wo_lo = sb("woa_lo", [P, DK, D], F32R)
        ot_hi = sb("ot_hi_a", [P, 2, DK, P], F32R)
        ot_lo = sb("ot_lo_a", [P, 2, DK, P], F32R)
        stats = sb("stats_oa", [P, 6])
        mv = sb("mv_oa", [P, 2])
        rs = sb("rs_oa", [P, 1])
        yn = sb("yn_oa", [P, D])
        pt = st.enter_context(nc.psum_tensor("pt_oa", [P, 2, CH], F32))
        py = st.enter_context(nc.psum_tensor("py_oa", [P, 2, CH], F32))
        w_loaded, w_high, w_split = core.sem("oa_w_loaded"), core.sem("oa_w_high"), core.sem("oa_w_split")
        turned, hi_done, lo_done = core.sem("oa_turned"), core.sem("oa_hi"), core.sem("oa_lo")
        y_done, y_out, chained = core.sem("oa_y_done"), core.sem("oa_y_out"), core.sem("oa_chained")
        rooted = core.sem("oa_rooted")
        with nc.Block() as block:
            @block.sync
            def _(sp):
                core.open_semaphores(sp)
                sp.dma_start(wo[:], woa_in).then_inc(w_loaded, 16)

            @block.tensor
            def _(pe):
                def turn(t):
                    if t >= 2:
                        pe.wait_ge(lo_done, t)
                    for dk in range(DK):
                        last = nc.tensor.transpose(pt[:, t % 2, dk * P:(dk + 1) * P],
                                                   O_all[:, t, dk * P:(dk + 1) * P], core.ident[:])
                    last.then_inc(turned, 1)
                turn(0)
                for t in range(NT):
                    if t + 1 < NT:
                        turn(t + 1)
                    if t == 0:
                        pe.wait_ge(w_split, 2)
                    pe.wait_ge(lo_done, t + 2)
                    if t >= 2:
                        pe.wait_ge(y_out, t)
                    for dk in range(DK):
                        last = three_products(nc, py[:, t % 2, 0:D], ot_hi[:, t % 2, dk, :], ot_lo[:, t % 2, dk, :],
                                              wo_hi[:, dk, :], wo_lo[:, dk, :], dk == 0, dk == DK - 1)
                    last.then_inc(y_done, 1)

            @block.scalar
            def _(act):
                act.wait_ge(w_loaded, 17)
                nc.scalar.activation(wo_hi[:], wo[:], ACT.Copy).then_inc(w_high, 1)

                def high(t):
                    act.wait_ge(turned, t + 2)
                    if t >= 2:
                        act.wait_ge(y_done, t)
                    nc.scalar.activation(ot_hi[:, t % 2, :, :], pt[:, t % 2, 0:D].rearrange("p (k t) -> p k t", k=DK),
                                         ACT.Copy).then_inc(hi_done, 1)
                high(0)
                for t in range(NT):
                    if t + 1 < NT:
                        high(t + 1)
                    root(core, act, rs[:], mv[:, 1:2], chained, 4 * t + 2, rooted)

            @block.vector
            def _(dve):
                dve.wait_ge(w_high, 2)
                nc.vector.tensor_tensor(wo_lo[:], wo[:], wo_hi[:], ALU.subtract).then_inc(w_split, 1)
                chain = Chain(dve, chained, core.passed)

                def low(t):
                    dve.wait_ge(hi_done, t + 2)
                    nc.vector.tensor_tensor(ot_lo[:, t % 2, :, :],
                                            pt[:, t % 2, 0:D].rearrange("p (k t) -> p k t", k=DK),
                                            ot_hi[:, t % 2, :, :], ALU.subtract).then_inc(lo_done, 1)
                low(0)
                for t in range(NT):
                    if t + 1 < NT:
                        low(t + 1)
                    dve.wait_ge(y_done, t + 2)
                    y = py[:, t % 2, 0:D]
                    chain.link(nc.vector.bn_stats(stats[:], y))
                    chain.link(nc.vector.bn_aggr(mv[:], stats[:]))
                    dve.wait_ge(rooted, t + 2)
                    chain.link(nc.vector.reciprocal(rs[:], rs[:]))
                    ins = nc.vector.tensor_scalar(yn[:], y, mv[:, 0:1], rs[:], ALU.subtract, ALU.mult)
                    ins.then_inc(y_out, 1)
                    dve.wait_ge(y_out, t + 2)
                    chain.link(nc.vector.tensor_tensor(core.X[:, t, :], core.X[:, t, :], yn[:], ALU.add))


def phase_project_b(core, hT, wq_in, wkv_in, cos_in, sin_in):
    nc = core.nc
    hT_hi, hT_lo = hT
    NH = HB + KVB
    HALF = P // 2
    NWC = (HB + 2 * KVB) * HDB
    with ExitStack() as st:
        sb = phase_sbuf(nc, st)
        w_raw = sb("wb_raw", [P, 2, 4, P])
        w_hi = sb("wb_hi", [P, DK, NWC], F32R)
        w_lo = sb("wb_lo", [P, DK, NWC], F32R)
        cos = sb("cos_b", [P, T])
        sin = sb("sin_b", [P, T])
        sw = sb("sw_b", [P, 2, CH])
        tc = sb("tc_b", [P, 2, CH])
        ts = sb("ts_b", [P, 2, CH])
        r = sb("r_b", [P, 2, CH])
        v_hi = sb("v_hi_b", [P, 2, KVB * HDB], F32R)
        v_lo = sb("v_lo_b", [P, 2, KVB * HDB], F32R)
        ps = st.enter_context(nc.psum_tensor("ps_pb", [P, 4, CH], F32))
        loaded = [core.sem(f"pb_loaded{i}") for i in range(2)]
        tab_loaded = core.sem("pb_tab")
        w_high, w_low = core.sem("pb_w_high"), core.sem("pb_w_low")
        projected, cos_done, swapped = core.sem("pb_projected"), core.sem("pb_cos_done"), core.sem("pb_swapped")
        sin_done, r_done = core.sem("pb_sin_done"), core.sem("pb_r_done")
        stored = [core.sem(f"pb_stored{i}") for i in range(2)]
        v_done, v_high, v_low = core.sem("pb_v_done"), core.sem("pb_v_high"), core.sem("pb_v_low")
        v_stored = [core.sem(f"pb_v_stored{i}") for i in range(2)]
        WT = NWC // CH
        pieces = [(dk, w) for dk in range(DK) for w in range(WT)]
        with nc.Block() as block:
            @block.sync
            def _(sp):
                core.open_semaphores(sp)
                sp.dma_start(cos[:], cos_in).then_inc(tab_loaded, 16)
                sp.dma_start(sin[:], sin_in).then_inc(tab_loaded, 16)
                for n, (dk, w) in enumerate(pieces):
                    if n >= 2:
                        sp.wait_ge(w_low, n)
                    sp.dma_start(w_raw[:, n % 2, :, :], wq_in[:, dk, w * 4:(w + 1) * 4, :]).then_inc(loaded[n % 2], 16)
                with sp.Fori(0, NC) as c:
                    for h in range(NH):
                        sp.wait_ge(r_done, c * NH + h + 2)
                        dst = core.q_b[h] if h < HB else core.k_b[h - HB]
                        sp.dma_start(dst[:, bass.ds(c * CH, CH)], r[:, h % 2, :]).then_inc(stored[h % 2], 16)
                for t in range(NT):
                    for part, buf, done in ((0, v_hi, v_high), (1, v_lo, v_low)):
                        sp.wait_ge(done, t + 2)
                        sp.dma_start(core.v_b[:, part, :, t, :].rearrange("g p d -> p g d"),
                                     raw(buf[:, t % 2, :]).rearrange("p (g d) -> p g d", g=KVB)).then_inc(v_stored[t % 2], 16)
                for i in range(2):
                    sp.wait_ge(stored[i], NH // 2 * NC * 16 + 1)
                    sp.wait_ge(v_stored[i], NT // 2 * 32 + 1)

            @block.tensor
            def _(pe):
                pe.wait_ge(w_low, len(pieces) + 1)
                with pe.Fori(0, NC) as c:
                    for h in range(NH):
                        if h >= 4:
                            pe.wait_ge(cos_done, c * NH + h - 3 + 1)
                            pe.wait_ge(swapped, c * NH + h - 3 + 1)
                        else:
                            pe.wait_ge(cos_done, c * NH + 1)
                            pe.wait_ge(swapped, c * NH + 1)
                        for dk in range(DK):
                            last = three_products(
                                nc, ps[:, h % 4, :], w_hi[:, dk, h * P:(h + 1) * P], w_lo[:, dk, h * P:(h + 1) * P],
                                hT_hi[:, dk, bass.ds(c * CH, CH)], hT_lo[:, dk, bass.ds(c * CH, CH)],
                                dk == 0, dk == DK - 1)
                        last.then_inc(projected, 1)
                pe.wait_ge(cos_done, NC * NH + 1)
                pe.wait_ge(swapped, NC * NH + 1)
                for t in range(NT):
                    if t >= 2:
                        pe.wait_ge(v_low, t)
                    for dk in range(DK):
                        last = three_products(nc, ps[:, t % 2, :],
                                              hT_hi[:, dk, t * P:(t + 1) * P], hT_lo[:, dk, t * P:(t + 1) * P],
                                              w_hi[:, dk, NH * P:NWC], w_lo[:, dk, NH * P:NWC],
                                              dk == 0, dk == DK - 1)
                    last.then_inc(v_done, 1)

            @block.scalar
            def _(act):
                for n, (dk, w) in enumerate(pieces):
                    act.wait_ge(loaded[n % 2], (n // 2 + 1) * 16 + 1)
                    nc.scalar.activation(w_hi[:, dk, w * CH:(w + 1) * CH],
                                         w_raw[:, n % 2, :, :].rearrange("p a b -> p (a b)"), ACT.Copy).then_inc(w_high, 1)
                with act.Fori(0, NC) as c:
                    for h in range(NH):
                        act.wait_ge(projected, c * NH + h + 2)
                        if h >= 2:
                            act.wait_ge(sin_done, c * NH + h)
                        else:
                            act.wait_ge(sin_done, c * NH + 1)
                        nc.scalar.activation(sw[0:HALF, h % 2, :], ps[HALF:P, h % 4, :], ACT.Copy)
                        nc.scalar.activation(sw[HALF:P, h % 2, :], ps[0:HALF, h % 4, :], ACT.Copy).then_inc(swapped, 1)
                for t in range(NT):
                    act.wait_ge(v_done, t + 2)
                    if t >= 2:
                        act.wait_ge(v_stored[t % 2], (t // 2) * 32 + 1)
                    nc.scalar.activation(v_hi[:, t % 2, :], ps[:, t % 2, :], ACT.Copy).then_inc(v_high, 1)

            @block.gpsimd
            def _(pool):
                pool.wait_ge(tab_loaded, 33)
                with pool.Fori(0, NC) as c:
                    for h in range(NH):
                        if h >= 2:
                            pool.wait_ge(r_done, c * NH + h)
                        else:
                            pool.wait_ge(r_done, c * NH + 1)
                        wait_apart(pool, swapped, c * NH + h + 1, core.passed)
                        nc.gpsimd.tensor_tensor(ts[:, h % 2, :], sw[:, h % 2, :], sin[:, bass.ds(c * CH, CH)],
                                                ALU.mult).then_inc(sin_done, 1)

            @block.vector
            def _(dve):
                for n, (dk, w) in enumerate(pieces):
                    dve.wait_ge(w_high, n + 2)
                    nc.vector.tensor_tensor(w_lo[:, dk, w * CH:(w + 1) * CH],
                                            w_raw[:, n % 2, :, :].rearrange("p a b -> p (a b)"),
                                            w_hi[:, dk, w * CH:(w + 1) * CH], ALU.subtract).then_inc(w_low, 1)
                dve.wait_ge(tab_loaded, 33)
                with dve.Fori(0, NC) as c:
                    def cosine(h):
                        dve.wait_ge(swapped, c * NH + h + 2)
                        nc.vector.tensor_tensor(tc[:, h % 2, :], ps[:, h % 4, :], cos[:, bass.ds(c * CH, CH)],
                                                ALU.mult).then_inc(cos_done, 1)
                    dve.wait_ge(r_done, c * NH + 1)
                    cosine(0)
                    for h in range(NH):
                        if h + 1 < NH:
                            dve.wait_ge(r_done, c * NH + h + 1)
                            cosine(h + 1)
                        dve.wait_ge(sin_done, c * NH + h + 2)
                        dve.wait_ge(cos_done, c * NH + h + 2)
                        if h >= 2:
                            dve.wait_ge(stored[h % 2], c * (NH // 2 * 16) + (h // 2) * 16 + 1)
                        else:
                            dve.wait_ge(stored[h % 2], c * (NH // 2 * 16) + 1)
                        nc.vector.tensor_tensor(r[:, h % 2, :], tc[:, h % 2, :], ts[:, h % 2, :],
                                                ALU.add).then_inc(r_done, 1)
                for t in range(NT):
                    dve.wait_ge(v_high, t + 2)
                    if t >= 2:
                        dve.wait_ge(v_stored[t % 2], (t // 2) * 32 + 1)
                    nc.vector.tensor_tensor(v_lo[:, t % 2, :], ps[:, t % 2, :], v_hi[:, t % 2, :],
                                            ALU.subtract).then_inc(v_low, 1)


def phase_attention_b(core):
    nc = core.nc
    LEAD = 3
    slots = [TPC * (i + 1) + 1 for i in range(NC)]
    slot0 = [sum(slots[:i]) for i in range(NC)]
    SLOTS = sum(slots)
    tiles0 = [TPC * sum(j + 1 for j in range(i)) for i in range(NC)]
    TILES = TPC * sum(j + 1 for j in range(NC))
    parts = [1, 1, 2, 2]
    part0 = [TPC * sum(parts[:i]) for i in range(NC)]
    PARTS = TPC * sum(parts)
    with ExitStack() as st:
        sb = phase_sbuf(nc, st)
        k_raw = sb("k_raw", [P, T])
        k_hi = sb("k_hi", [P, T], F32R)
        k_lo = sb("k_lo", [P, T], F32R)
        v_hi = sb("v_hi", [P, NT, HDB], F32R)
        v_lo = sb("v_lo", [P, NT, HDB], F32R)
        q_raw = sb("q_raw", [P, 2, CH])
        q_hi = sb("q_hi", [P, 2, CH], F32R)
        q_lo = sb("q_lo", [P, 2, CH], F32R)
        p = sb("p_b", [P, 2, TPC, T])
        pT_hi = sb("pT_hi", [P, 3, CH], F32R)
        pT_lo = sb("pT_lo", [P, 3, CH], F32R)
        mx = sb("mx_b", [P, 4, 2])
        bias = sb("bias_b", [P, 2, TPC])
        rsum = sb("rsum_b", [P, 2, TPC])
        rrec = sb("rrec_b", [P, TPC])
        diag = sb("diag_b", [P, TPC, P])
        r_sb = sb("r_sb_b", [P, CH])
        o_sb = sb("o_sb_b", [P, 2, CH])
        ps = st.enter_context(nc.psum_tensor("ps_ab", [P, T], F32))
        pt = st.enter_context(nc.psum_tensor("pt_ab", [P, 3, CH], F32))
        po = st.enter_context(nc.psum_tensor("po_ab", [P, CH], F32))
        k_loaded, v_loaded = core.sem("ab_k_loaded"), core.sem("ab_v_loaded")
        q_loaded = [core.sem(f"ab_q_loaded{i}") for i in range(2)]
        k_high, k_low, q_high, q_low = (core.sem(f"ab_{n}") for n in ("k_high", "k_low", "q_high", "q_low"))
        scored, maxed, biased, exped = (core.sem(f"ab_{n}") for n in ("scored", "maxed", "biased", "exped"))
        turned, high, low, valued = (core.sem(f"ab_{n}") for n in ("turned", "high", "low", "valued"))
        inverted, diagonal, spread, spread_out = (core.sem(f"ab_{n}") for n in ("inverted", "diagonal", "spread", "spread_out"))
        o_ready = core.sem("ab_o_ready")
        o_stored = [core.sem(f"ab_o_stored{i}") for i in range(2)]

        def beside(i):
            rows = range(TPC) if i < NC else ()
            tiles = TPC * i
            early = 1 if i == 1 else 0
            order = [("row", 0)] * early
            turned_to = 0
            for r in range(TPC):
                while turned_to < min(tiles, r * i + LEAD):
                    order.append(("turn", turned_to))
                    turned_to += 1
                if r in rows and r >= early:
                    order.append(("row", r))
                for k in range(r * i, (r + 1) * i):
                    order.append(("product", k))
                    if turned_to < tiles:
                        order.append(("turn", turned_to))
                        turned_to += 1
            return order

        def heads(eng, group, head):
            with eng.Fori(0, KVB) as g:
                group(g)
                with eng.Fori(0, REP) as hh:
                    head(g, g * REP + hh)

        with nc.Block() as block:
            @block.sync
            def _(sp):
                core.open_semaphores(sp)
                def group(g):
                    sp.wait_ge(k_low, g + 1)
                    sp.dma_start(k_raw[:], core.k_b[bass.ds(g, 1), :, :].rearrange("a p t -> (a p) t")).then_inc(k_loaded, 16)
                    sp.wait_ge(valued, g * (REP * TILES) + 1)
                    for part, buf in ((0, v_hi), (1, v_lo)):
                        sp.dma_start(raw(buf[:]), core.v_b[bass.ds(g, 1), part, :, :, :].rearrange("a p t d -> (a p) t d")).then_inc(v_loaded, 16)

                def head(g, h):
                    for i in range(NC):
                        if i >= 2:
                            sp.wait_ge(q_low, h * NC + i)
                        else:
                            sp.wait_ge(q_low, h * NC + 1)
                        src = core.q_b[bass.ds(h, 1), :, i * CH:(i + 1) * CH].rearrange("a p t -> (a p) t")
                        sp.dma_start(q_raw[:, i % 2, :], src).then_inc(q_loaded[i % 2], 16)
                heads(sp, group, head)
                for i in range(2):
                    sp.wait_ge(o_stored[i], HB * NC // 2 * 16 + 1)

            @block.gpsimd
            def _(pool):
                def head(g, h):
                    for i in range(NC):
                        pool.wait_ge(spread, h * NC + i + 1)
                        wait_apart(pool, inverted, h * NC + i + 1, core.passed)
                        for r in range(TPC):
                            last = nc.gpsimd.tensor_scalar(diag[:, r, :], core.ident[:], rrec[:, r:r + 1], None, ALU.mult)
                        last.then_inc(diagonal, 1)
                heads(pool, lambda g: None, head)

            @block.tensor
            def _(pe):
                def group(g):
                    wait_apart(pe, k_low, g + 1, core.passed)

                def head(g, h):
                    def row(i, r):
                        if r == 0:
                            pe.wait_ge(q_low, h * NC + i + 2)
                        before = h * NT + i * TPC
                        if i == 0:
                            pe.wait_ge(exped, before + 1)
                        elif i == 1:
                            pe.wait_ge(exped, (before - TPC + 2 * r + 2 if r < 2 else before + r - 1) + 1)
                        else:
                            pe.wait_ge(exped, before + r + 1)
                        b0 = r * CH if i == 0 else (r % 2) * 2 * CH if i == 1 else 0
                        for c in range(i + 1):
                            w = CH if c < i else (r + 1) * P
                            wide = max(w, 2 * P)
                            out = ps[:, b0 + c * CH:b0 + c * CH + wide]
                            last = three_products(nc, out, q_hi[:, i % 2, r * P:(r + 1) * P],
                                                  q_lo[:, i % 2, r * P:(r + 1) * P],
                                                  k_hi[:, c * CH:c * CH + wide], k_lo[:, c * CH:c * CH + wide],
                                                  True, c < i)
                            if c == i:
                                e = b0 + c * CH + w
                                last = nc.tensor.matmul(ps[:, e - P:e], core.identb[:], core.maskq[:],
                                                        start=False, stop=True, skip_group_check=True)
                            if c == i or (i >= 2 and c == 1):
                                last.then_inc(scored, 1)

                    def turn(i, kt):
                        n = slot0[i] + kt
                        if kt == 0:
                            pe.wait_ge(exped, h * NT + (i + 1) * TPC + 1)
                        if n < 3:
                            pe.wait_ge(spread_out, h * NC + 1)
                        elif kt < 3:
                            pe.wait_ge(spread_out, h * NC + i + 1)
                        g = max(0, kt - i * TPC)
                        for r in range(g, TPC):
                            last = nc.tensor.transpose(pt[:, n % 3, r * P:(r + 1) * P],
                                                       p[:, i % 2, r, kt * P:(kt + 1) * P], core.ident[:])
                        last.then_inc(turned, 1)

                    def product(i, kt):
                        n = tiles0[i] + kt
                        g = max(0, kt - i * TPC)
                        pe.wait_ge(low, h * TILES + n + 2)
                        pe.wait_ge(high, h * TILES + n + 2)
                        if i == 0 and kt == 0:
                            pe.wait_ge(v_loaded, (g0 + 1) * 32 + 1)
                        if kt == 0:
                            pe.wait_ge(o_ready, h * NC + i + 1)
                        last = three_products(nc, po[:, g * P:], v_hi[:, kt, :], v_lo[:, kt, :],
                                              pT_hi[:, n % 3, g * P:], pT_lo[:, n % 3, g * P:],
                                              kt == 0, kt == TPC * (i + 1) - 1)
                        last.then_inc(valued, 1)

                    def finish(i):
                        pe.wait_ge(diagonal, h * NC + i + 2)
                        n = slot0[i] + TPC * (i + 1)
                        nc.tensor.matmul(pt[:, n % 3, :], core.ones[:], diag[:].rearrange("p r q -> p (r q)"),
                                         start=True, stop=True, skip_group_check=True).then_inc(spread, 1)

                    g0 = g
                    for i in range(NC + 1):
                        for what, n in beside(i):
                            if what == "row":
                                row(i, n)
                            elif what == "turn":
                                turn(i - 1, n)
                            else:
                                product(i - 1, n)
                        if i >= 1:
                            finish(i - 1)
                heads(pe, group, head)

            @block.scalar
            def _(act):
                def group(g):
                    act.wait_ge(k_loaded, (g + 1) * 16 + 1)
                    act.wait_ge(scored, g * (REP * PARTS) + 1)
                    nc.scalar.activation(k_hi[:], k_raw[:], ACT.Copy).then_inc(k_high, 1)

                def head(g, h):
                    def q_split(i):
                        act.wait_ge(q_loaded[i % 2], h * (NC // 2 * 16) + (i // 2 + 1) * 16 + 1)
                        if i >= 2:
                            act.wait_ge(scored, h * PARTS + part0[i - 1] + 1)
                        else:
                            act.wait_ge(scored, h * PARTS + 1)
                        nc.scalar.activation(q_hi[:, i % 2, :], q_raw[:, i % 2, :], ACT.Copy).then_inc(q_high, 1)

                    def exp_row(i, r):
                        act.wait_ge(biased, h * NT + i * TPC + r + 2)
                        if i >= 2:
                            act.wait_ge(turned, h * TILES + tiles0[i - 1] + 1)
                        else:
                            act.wait_ge(turned, h * TILES + 1)
                        if i >= 2:
                            act.wait_ge(inverted, h * NC + i)
                        else:
                            act.wait_ge(inverted, h * NC + 1)
                        b0 = r * CH if i == 0 else (r % 2) * 2 * CH if i == 1 else 0
                        w = (i * TPC + r + 1) * P
                        nc.scalar.activation(p[:, i % 2, r, 0:w], ps[:, b0:b0 + w], ACT.Exp,
                                             bias=bias[:, i % 2, r:r + 1], scale=SCALE_B,
                                             accum_out=rsum[:, i % 2, r:r + 1]).then_inc(exped, 1)

                    def high_part(i, kt):
                        n = tiles0[i] + kt
                        g = max(0, kt - i * TPC)
                        act.wait_ge(turned, h * TILES + n + 2)
                        act.wait_ge(valued, h * TILES + max(0, n - 2) + 1)
                        nc.scalar.activation(pT_hi[:, n % 3, g * P:], pt[:, (slot0[i] + kt) % 3, g * P:],
                                             ACT.Copy).then_inc(high, 1)

                    def spread_copy(i):
                        act.wait_ge(spread, h * NC + i + 2)
                        act.wait_ge(o_ready, h * NC + i + 1)
                        nc.scalar.activation(r_sb[:], pt[:, (slot0[i] + TPC * (i + 1)) % 3, :],
                                             ACT.Copy).then_inc(spread_out, 1)

                    def store(i):
                        act.wait_ge(o_ready, h * NC + i + 2)
                        dst = core.o_b[:, bass.ds(h, 1), i * CH:(i + 1) * CH].rearrange("p a t -> p (a t)")
                        act.dma_start(dst, o_sb[:, i % 2, :]).then_inc(o_stored[i % 2], 16)

                    q_split(0)
                    for i in range(NC + 1):
                        for what, n in beside(i):
                            if what == "row":
                                exp_row(i, n)
                                if n == 0 and i + 1 < NC:
                                    q_split(i + 1)
                                if n == 1 and i >= 2:
                                    store(i - 2)
                            elif what == "turn":
                                high_part(i - 1, n)
                                if i == NC and n == LEAD:
                                    store(NC - 2)
                        if i >= 1:
                            spread_copy(i - 1)
                    store(NC - 1)
                heads(act, group, head)

            @block.vector
            def _(dve):
                def group(g):
                    dve.wait_ge(k_high, g + 2)
                    nc.vector.tensor_tensor(k_lo[:], k_raw[:], k_hi[:], ALU.subtract).then_inc(k_low, 1)

                def head(g, h):
                    def q_split(i):
                        dve.wait_ge(q_high, h * NC + i + 2)
                        nc.vector.tensor_tensor(q_lo[:, i % 2, :], q_raw[:, i % 2, :], q_hi[:, i % 2, :],
                                                ALU.subtract).then_inc(q_low, 1)

                    def max_row(i, r):
                        b0 = r * CH if i == 0 else (r % 2) * 2 * CH if i == 1 else 0
                        w = (i * TPC + r + 1) * P
                        s0 = h * PARTS + part0[i] + r * parts[i]
                        cuts = [0, w] if parts[i] == 1 else [0, 2 * CH, w]
                        for k in range(parts[i]):
                            dve.wait_ge(scored, s0 + k + 2)
                            last = nc.vector.tensor_reduce(mx[:, r, k:k + 1], ps[:, b0 + cuts[k]:b0 + cuts[k + 1]],
                                                           axis=AX.X, op=ALU.max, negate=True)
                            last.then_inc(maxed, 1)
                        dve.wait_ge(maxed, s0 + parts[i] + 1)
                        other = mx[:, r, 1:2] if parts[i] == 2 else mx[:, r, 0:1]
                        if i < 2:
                            dve.wait_ge(exped, h * NT + i * TPC + 1)
                        nc.vector.tensor_scalar(bias[:, i % 2, r:r + 1], mx[:, r, 0:1], other, SCALE_B,
                                                ALU.min, ALU.mult).then_inc(biased, 1)

                    def low_part(i, kt):
                        n = tiles0[i] + kt
                        g = max(0, kt - i * TPC)
                        dve.wait_ge(high, h * TILES + n + 2)
                        nc.vector.tensor_tensor(pT_lo[:, n % 3, g * P:], pt[:, (slot0[i] + kt) % 3, g * P:],
                                                pT_hi[:, n % 3, g * P:], ALU.subtract).then_inc(low, 1)

                    def invert(i):
                        dve.wait_ge(exped, h * NT + (i + 1) * TPC + 1)
                        dve.wait_ge(diagonal, h * NC + i + 1)
                        nc.vector.reciprocal(rrec[:], rsum[:, i % 2, :]).then_inc(inverted, 1)

                    def output(i):
                        dve.wait_ge(spread_out, h * NC + i + 2)
                        if i >= 2:
                            dve.wait_ge(o_stored[i % 2], h * (NC // 2 * 16) + (i // 2) * 16 + 1)
                        else:
                            dve.wait_ge(o_stored[i % 2], h * (NC // 2 * 16) + 1)
                        nc.vector.tensor_tensor(o_sb[:, i % 2, :], po[:], r_sb[:], ALU.mult).then_inc(o_ready, 1)

                    q_split(0)
                    for i in range(NC + 1):
                        if i == NC:
                            invert(NC - 1)
                        for what, n in beside(i):
                            if what == "row":
                                max_row(i, n)
                                if n == 0 and i + 1 < NC:
                                    q_split(i + 1)
                                if n == 0 and i >= 1:
                                    invert(i - 1)
                            elif what == "turn":
                                low_part(i - 1, n)
                        if i >= 1:
                            output(i - 1)
                heads(dve, group, head)


def phase_output_b(core, wob_in):
    nc = core.nc
    with ExitStack() as st:
        sb = phase_sbuf(nc, st)
        wo = sb("wob", [P, HB, D])
        wo_hi = sb("wob_hi", [P, HB, D], F32R)
        wo_lo = sb("wob_lo", [P, HB, D], F32R)
        o_raw = [sb(f"o_raw{i}", [P, HB, P]) for i in range(2)]
        o_hi = [sb(f"o_hi{i}", [P, HB, P], F32R) for i in range(2)]
        o_lo = [sb(f"o_lo{i}", [P, HB, P], F32R) for i in range(2)]
        py = st.enter_context(nc.psum_tensor("py_ob", [P, 2, CH], F32))
        w_loaded, w_high, w_split = core.sem("ob_w_loaded"), core.sem("ob_w_high"), core.sem("ob_w_split")
        loaded = [core.sem(f"ob_loaded{i}") for i in range(2)]
        hi_done, lo_done, y_done, y_out = (core.sem(f"ob_{n}") for n in ("hi", "lo", "y_done", "y_out"))
        with nc.Block() as block:
            @block.sync
            def _(sp):
                core.open_semaphores(sp)
                sp.dma_start(wo[:], wob_in).then_inc(w_loaded, 16)
                with sp.Fori(0, NT // 2) as j:
                    for i in range(2):
                        sp.wait_ge(lo_done, (2 * j + i - 1 if i == 1 else 2 * j) + 1)
                        sp.dma_start(o_raw[i][:], core.o_b[:, :, bass.ds((2 * j + i) * P, P)]).then_inc(loaded[i], 16)

            @block.tensor
            def _(pe):
                pe.wait_ge(w_split, 2)
                with pe.Fori(0, NT // 2) as j:
                    for i in range(2):
                        pe.wait_ge(lo_done, 2 * j + i + 2)
                        pe.wait_ge(y_out, (2 * j + i - 1 if i == 1 else 2 * j) + 1)
                        for h in range(HB):
                            last = three_products(nc, py[:, i, 0:D], o_hi[i][:, h, :], o_lo[i][:, h, :],
                                                  wo_hi[:, h, :], wo_lo[:, h, :], h == 0, h == HB - 1)
                        last.then_inc(y_done, 1)

            @block.scalar
            def _(act):
                act.wait_ge(w_loaded, 17)
                nc.scalar.activation(wo_hi[:], wo[:], ACT.Copy).then_inc(w_high, 1)
                with act.Fori(0, NT // 2) as j:
                    for i in range(2):
                        act.wait_ge(loaded[i], (j + 1) * 16 + 1)
                        act.wait_ge(y_done, (2 * j + i - 1 if i == 1 else 2 * j) + 1)
                        nc.scalar.activation(o_hi[i][:], o_raw[i][:], ACT.Copy).then_inc(hi_done, 1)

            @block.vector
            def _(dve):
                dve.wait_ge(w_high, 2)
                nc.vector.tensor_tensor(wo_lo[:], wo[:], wo_hi[:], ALU.subtract).then_inc(w_split, 1)

                with dve.Fori(0, NT // 2) as j:
                    for i in range(2):
                        dve.wait_ge(hi_done, 2 * j + i + 2)
                        nc.vector.tensor_tensor(o_lo[i][:], o_raw[i][:], o_hi[i][:], ALU.subtract).then_inc(lo_done, 1)
                        if i == 1:
                            for k in range(2):
                                dve.wait_ge(y_done, 2 * j + k + 2)
                                rt = core.R[:, bass.ds(2 * j + k, 1), :].rearrange("p a d -> p (a d)")
                                nc.vector.tensor_tensor(rt, rt, py[:, k, 0:D], ALU.add).then_inc(y_out, 1)


def phase_experts(core, hT, gates, w13_in, w2_in):
    nc = core.nc
    hT_hi, hT_lo = hT
    SPLITS = 3
    with ExitStack() as st:
        sb = phase_sbuf(nc, st)
        w13 = sb("w13", [P, 2, DK, FF])
        w2 = sb("w2", [P, FT, D])
        w13_hi = sb("w13_hi", [P, 2, DK, FF], F32R)
        w13_lo = sb("w13_lo", [P, 2, DK, FF], F32R)
        w2_hi = sb("w2_hi", [P, FT, D], F32R)
        w2_lo = sb("w2_lo", [P, FT, D], F32R)
        s1 = sb("s1", [P, 2, CH])
        gu = sb("gu", [P, 2, CH])
        g_hi = sb("g_hi", [P, FT, CH], F32R)
        g_lo = sb("g_lo", [P, FT, CH], F32R)
        ph = st.enter_context(nc.psum_tensor("ph_e", [P, 2, 2, CH], F32))
        py = st.enter_context(nc.psum_tensor("py_e", [P, 4, CH], F32))
        loaded, high, low = core.sem("e_loaded"), core.sem("e_w_high"), core.sem("e_w_low")
        mixed, silued, gated, g_high, g_low = (core.sem(f"e_{n}") for n in ("mixed", "silued", "gated", "g_high", "g_low"))
        y_done, y_out = core.sem("e_y_done"), core.sem("e_y_out")

        def loops(eng, expert, chunk):
            with eng.Fori(0, NE) as e:
                expert(e)
                with eng.Fori(0, NC) as c:
                    chunk(e, c, e * NC + c)

        with nc.Block() as block:
            @block.sync
            def _(sp):
                core.open_semaphores(sp)
                with sp.Fori(0, NE) as e:
                    sp.wait_ge(low, e + 1)
                    sp.dma_start(w13[:], w13_in[bass.ds(e, 1)].rearrange("a p w k f -> (a p) w k f")).then_inc(loaded, 16)
                    sp.dma_start(w2[:], w2_in[bass.ds(e, 1)].rearrange("a p f d -> (a p) f d")).then_inc(loaded, 16)

            @block.tensor
            def _(pe):
                def expert(e):
                    wait_apart(pe, low, e + 1, core.passed)

                def chunk(e, c, n):
                    for f in range(FT):
                        pe.wait_ge(gated, (n * FT + f - 1 if f >= 2 else n * FT) + 1)
                        for w in range(2):
                            for dk in range(DK):
                                last = three_products(
                                    nc, ph[:, f % 2, w, :], w13_hi[:, w, dk, f * P:(f + 1) * P],
                                    w13_lo[:, w, dk, f * P:(f + 1) * P],
                                    hT_hi[:, dk, bass.ds(c * CH, CH)], hT_lo[:, dk, bass.ds(c * CH, CH)],
                                    dk == 0, dk == DK - 1)
                        last.then_inc(mixed, 1)
                    pe.wait_ge(g_low, (n + 1) * FT + 1)
                    for t in range(TPC):
                        pe.wait_ge(y_out, n * TPC + 1)
                        for f in range(FT):
                            last = three_products(nc, py[:, t, 0:D], g_hi[:, f, t * P:(t + 1) * P],
                                                  g_lo[:, f, t * P:(t + 1) * P], w2_hi[:, f, :], w2_lo[:, f, :],
                                                  f == 0, f == FT - 1)
                        last.then_inc(y_done, 1)
                loops(pe, expert, chunk)

            @block.scalar
            def _(act):
                def expert(e):
                    act.wait_ge(loaded, (e + 1) * 32 + 1)
                    act.wait_ge(y_done, e * (NC * TPC) + 1)
                    nc.scalar.activation(w13_hi[:], w13[:], ACT.Copy)
                    nc.scalar.activation(w2_hi[:], w2[:], ACT.Copy).then_inc(high, 1)

                def chunk(e, c, n):
                    for f in range(FT):
                        act.wait_ge(mixed, n * FT + f + 2)
                        act.wait_ge(gated, (n * FT + f - 1 if f >= 2 else n * FT) + 1)
                        nc.scalar.activation(s1[:, f % 2, :], ph[:, f % 2, 0, :], ACT.Silu).then_inc(silued, 1)
                        act.wait_ge(gated, n * FT + f + 2)
                        if f == 0:
                            act.wait_ge(y_done, n * TPC + 1)
                        nc.scalar.activation(g_hi[:, f, :], gu[:, f % 2, :], ACT.Copy).then_inc(g_high, 1)
                loops(act, expert, chunk)

            @block.vector
            def _(dve):
                def expert(e):
                    dve.wait_ge(high, e + 2)
                    nc.vector.tensor_tensor(w13_lo[:], w13[:], w13_hi[:], ALU.subtract)
                    nc.vector.tensor_tensor(w2_lo[:], w2[:], w2_hi[:], ALU.subtract).then_inc(low, 1)

                def chunk(e, c, n):
                    for f in range(FT):
                        dve.wait_ge(silued, n * FT + f + 2)
                        dve.wait_ge(g_low, (n * FT + f - 1 if f >= 2 else n * FT) + 1)
                        nc.vector.tensor_tensor(gu[:, f % 2, :], s1[:, f % 2, :], ph[:, f % 2, 1, :],
                                                ALU.mult).then_inc(gated, 1)
                        dve.wait_ge(g_high, n * FT + f + 2)
                        if f == 0:
                            dve.wait_ge(y_done, n * TPC + 1)
                        nc.vector.tensor_tensor(g_lo[:, f, :], gu[:, f % 2, :], g_hi[:, f, :],
                                                ALU.subtract).then_inc(g_low, 1)
                    for t in range(TPC):
                        dve.wait_ge(y_done, n * TPC + t + 2)
                        rt = core.R[:, bass.ds(c * TPC + t, 1), :].rearrange("p a d -> p (a d)")
                        gate = gates[:, bass.ds(c * TPC + t, 1), bass.ds(e, 1)].rearrange("p a b -> p (a b)")
                        nc.vector.scalar_tensor_tensor(rt, py[:, t, 0:D], gate, rt, ALU.mult, ALU.add).then_inc(y_out, 1)
                loops(dve, expert, chunk)


def phase_route(core, gates, tri_in):
    nc = core.nc
    with ExitStack() as st:
        sb = phase_sbuf(nc, st)
        tri = sb("tri", [P, NE, NE])
        gt = sb("gt", [P, NT, NE, NE])
        eq = sb("eq", [P, NT, NE, NE])
        rank = sb("rank", [P, NT, NE])
        top = sb("top", [P, NT, 1])
        ex = sb("ex", [P, NT, NE])
        tot = sb("tot", [P, NT, 1])
        loaded, chained, shifted, exped = (core.sem(f"rt_{n}") for n in ("loaded", "chained", "shifted", "exped"))
        with nc.Block() as block:
            @block.sync
            def _(sp):
                core.open_semaphores(sp)
                sp.dma_start(tri[:], tri_in).then_inc(loaded, 16)

            @block.scalar
            def _(act):
                act.wait_ge(shifted, 2)
                nc.scalar.activation(ex[:], gates[:], ACT.Exp).then_inc(exped, 1)

            @block.vector
            def _(dve):
                chain = Chain(dve, chained, core.passed)
                dve.wait_ge(loaded, 17)
                lg = core.logits
                chain.link(nc.vector.tensor_reduce(top[:], lg[:], axis=AX.X, op=ALU.max))
                nc.vector.tensor_tensor(gates[:], lg[:], top[:].broadcast_to([P, NT, NE]), ALU.subtract).then_inc(shifted, 1)
                for t in range(NT):
                    lj = lg[:, t:t + 1, :].broadcast_to([P, NE, NE])
                    le = lg[:, t, :].rearrange("p (e a) -> p e a", a=1).broadcast_to([P, NE, NE])
                    nc.vector.tensor_tensor(gt[:, t, :, :], lj, le, ALU.is_gt)
                    last = nc.vector.tensor_tensor(eq[:, t, :, :], lj, le, ALU.is_equal)
                chain.link(last)
                for t in range(NT):
                    last = nc.vector.tensor_tensor(eq[:, t, :, :], eq[:, t, :, :], tri[:], ALU.mult)
                chain.link(last)
                chain.link(nc.vector.tensor_tensor(gt[:], gt[:], eq[:], ALU.add))
                chain.link(nc.vector.tensor_reduce(rank[:], gt[:], axis=AX.X, op=ALU.add))
                chain.link(nc.vector.tensor_scalar(rank[:], rank[:], float(TOPK) - 0.5, None, ALU.is_lt))
                dve.wait_ge(exped, 2)
                chain.link(nc.vector.tensor_tensor(ex[:], ex[:], rank[:], ALU.mult))
                chain.link(nc.vector.tensor_reduce(tot[:], ex[:], axis=AX.X, op=ALU.add))
                chain.link(nc.vector.reciprocal(tot[:], tot[:]))
                chain.link(nc.vector.tensor_tensor(gates[:], ex[:], tot[:].broadcast_to([P, NT, NE]), ALU.mult))


def phase_final(core, out):
    nc = core.nc
    with ExitStack() as st:
        sb = phase_sbuf(nc, st)
        yn = sb("yn_f", [P, TPC, D])
        rooted, stored, chained = core.sem("f_rooted"), core.sem("f_stored"), core.sem("f_chained")
        with nc.Block() as block:
            @block.scalar
            def _(act):
                for c in range(NC):
                    root(core, act, core.rstd[:], core.mv[:, :, 1:2], chained, 5 * c + 2, rooted)

            @block.vector
            def _(dve):
                for c in range(NC):
                    chain = Chain(dve, chained, core.passed, 5 * c)
                    layer_norm_stats(nc, chain, core, lambda t: core.R[:, c * TPC + t, :], rooted, c + 1)
                    for t in range(TPC):
                        last = nc.vector.tensor_scalar(yn[:, t, :], core.R[:, c * TPC + t, :], core.mv[:, t, 0:1],
                                                       core.rstd[:, t, :], ALU.subtract, ALU.mult)
                    chain.link(last)
                    Xc = core.X[:, c * TPC:(c + 1) * TPC, :]
                    ins = nc.vector.tensor_tensor(Xc, Xc, yn[:], ALU.add)
                    chain.link(ins)

            @block.sync
            def _(sp):
                core.open_semaphores(sp)
                for c in range(NC):
                    sp.wait_ge(chained, 5 * (c + 1) + 1)
                    sp.dma_start(out[:, c * TPC:(c + 1) * TPC, :], core.X[:, c * TPC:(c + 1) * TPC, :]).then_inc(stored, 16)
                sp.wait_ge(stored, NC * 16 + 1)


def program(nc, x, ident, identb, maskq, maskt, wcol, cos_a, sin_a, cos_b, sin_b, wa, woa, wqkv, wob,
            gate, tri, w13, w2, out, stop=99, dbg=None):
    with ExitStack() as root:
        core = Core(nc, root)
        core.qk_a = core.scratch("qk_a", [2 * HA, 2, HDA, T])
        core.q_b = core.scratch("q_b", [HB, P, T])
        core.k_b = core.scratch("k_b", [KVB, P, T])
        core.v_b = core.scratch("v_b", [KVB, 2, P, NT, HDB])
        core.o_b = core.scratch("o_b", [P, HB, T])
        core.X = core.keep("X", [P, NT, D])
        core.R = core.keep("R", [P, NT, D])
        core.ident = core.keep("ident", [P, P])
        core.identb = core.keep("identb", [P, P], BF16)
        core.ones = core.keep("ones", [P, P])
        core.eps = core.keep("eps", [P, 1])
        core.maskq = core.keep("maskq", [P, P], BF16)
        core.maskt = core.keep("maskt", [P, 3 * P + CH], BF16)
        core.wcol = core.keep("wcol", [P, 3, DK])
        core.stats = core.keep("stats", [P, TPC, 6])
        core.mv = core.keep("mv", [P, TPC, 2])
        core.rstd = core.keep("rstd", [P, TPC, 1])
        core.logits = core.keep("logits", [P, NT, NE])
        gates = core.keep("gates", [P, NT, NE])
        gate_w = core.keep("gate_w", [P, DK, NE])

        def load(sp, loaded):
            for dst, src in ((core.X, x), (core.ident, ident), (core.identb, identb), (core.maskq, maskq),
                             (core.maskt, maskt), (core.wcol, wcol), (gate_w, gate)):
                sp.dma_start(dst[:], src).then_inc(loaded, 16)
        load.count = 7

        def hT_buffers(stack, tag):
            sb = phase_sbuf(nc, stack)
            return sb(f"hT_hi_{tag}", [P, DK, T], F32R), sb(f"hT_lo_{tag}", [P, DK, T], F32R)

        with ExitStack() as st:
            sb = phase_sbuf(nc, st)
            V_all = sb("V_all", [P, NT, D])
            O_all = sb("O_all", [P, NT, D])
            with ExitStack() as st1:
                hT = hT_buffers(st1, "a")
                phase_norm(core, "a", "ln", hT, load=load)
                phase_project_a(core, hT, V_all, wa, cos_a, sin_a)
            phase_attention_a(core, V_all, O_all)
            phase_output_a(core, O_all, woa)
        with ExitStack() as st:
            hT = hT_buffers(st, "b")
            phase_norm(core, "b", "ln_rms", hT)
            phase_project_b(core, hT, wqkv, None, cos_b, sin_b)
        phase_attention_b(core)
        phase_output_b(core, wob)
        with ExitStack() as st:
            hT = hT_buffers(st, "m")
            phase_norm(core, "m", "rms", hT, gate=gate_w)
            phase_route(core, gates, tri)
            phase_experts(core, hT, gates, w13, w2)
        phase_final(core, out)


def shape_constants():
    f = np.float32
    pos = np.arange(T, dtype=f)
    half = HDA // 2
    inv_a = (f(1.0) / np.power(f(10000.0), np.arange(0, HDA, 2, dtype=f) / f(HDA))).astype(f)
    ang_a = (pos[None, :] * inv_a[:, None]).astype(f)
    cos_a = np.tile(np.cos(ang_a).astype(f), (2 * HPT, 1))
    sin_a = np.tile(np.concatenate([-np.sin(ang_a), np.sin(ang_a)]).astype(f), (HPT, 1))
    inv_b = np.power(f(1000000.0), -np.arange(0, HDB, 2, dtype=f) / f(HDB)).astype(f)
    ang_b = (pos[None, :] * inv_b[:, None]).astype(f)
    cos_b = np.concatenate([np.cos(ang_b)] * 2).astype(f)
    sin_b = np.concatenate([-np.sin(ang_b), np.sin(ang_b)]).astype(f)
    bf = mybir.dt.np(BF16)
    i = np.arange(P)
    maskq = np.where(i[None, :] > i[:, None], NEG, 0.0).astype(bf)
    c = np.arange(3 * P + CH) - 3 * P
    maskt = np.where(c[None, :] < i[:, None], NEG, 0.0).astype(bf)
    e = np.arange(NE)
    tri = np.broadcast_to((e[None, :] < e[:, None]).astype(f), (P, NE, NE))
    return dict(ident=np.eye(P, dtype=f), identb=np.eye(P, dtype=f).astype(bf), maskq=maskq, maskt=maskt,
                cos_a=cos_a, sin_a=sin_a, cos_b=cos_b, sin_b=sin_b, tri=np.ascontiguousarray(tri))


def layouts(i):
    def rows(w):
        w = np.asarray(w)
        return np.ascontiguousarray(w.reshape(-1, P, w.shape[-1]).transpose(1, 0, 2))

    wqkv = np.asarray(i["L0_attn_w_qkv"])
    qk = wqkv[:, :2 * D].reshape(D, 2 * HA, 2, HDA // 2)
    swapped = qk[:, :, ::-1, :].reshape(D, 2 * D)

    def pairs(w, n):
        return np.asarray(w).reshape(D, n, HDB // 2, 2).transpose(0, 1, 3, 2).reshape(D, n * HDB)

    wb = np.concatenate([pairs(i["L0_ffn_wq"], HB), pairs(i["L0_ffn_wk"], KVB), np.asarray(i["L0_ffn_wv"])], axis=1)
    w1, w3, w2 = (np.asarray(i[f"L0_ffn_{n}"]) for n in ("w1", "w3", "w2"))
    w13 = np.stack([w1, w3], axis=1).reshape(NE, 2, DK, P, FF).transpose(0, 3, 1, 2, 4)
    ones = np.ones((D,), np.float32)
    wcol = np.stack([ones, np.asarray(i["L0_ffn_ln_w"]), np.asarray(i["L0_ffn_ff_ln_w"])])
    return dict(
        x=rows(np.asarray(i["L0_attn_x"])[0]),
        wcol=np.ascontiguousarray(wcol.reshape(3, DK, P).transpose(2, 0, 1)),
        wa=rows(np.concatenate([wqkv, swapped], axis=1)),
        woa=rows(i["L0_attn_w_o"]),
        wqkv=np.ascontiguousarray(rows(wb).reshape(P, DK, HB + 2 * KVB, HDB)),
        wob=rows(i["L0_ffn_wo"]),
        gate=rows(i["L0_ffn_gate_w"]),
        w13=np.ascontiguousarray(w13),
        w2=np.ascontiguousarray(w2.reshape(NE, FT, P, D).transpose(0, 2, 1, 3)),
    )


def kernel(**inputs):
    import concourse.bacc as bacc
    from concourse.bass_utils import run_bass_kernel_spmd

    nc = bacc.Bacc("TRN2", target_bir_lowering=False, num_devices=1)
    arrays = {**layouts(inputs), **shape_constants()}
    args = {n: nc.dram_tensor(f"in_{n}", a.shape, mybir.dt.from_np(a.dtype), kind="ExternalInput").ap()
            for n, a in arrays.items()}
    out = nc.dram_tensor("out", [P, NT, D], F32, kind="ExternalOutput").ap()
    program(nc, out=out, **args)
    r = run_bass_kernel_spmd(nc, [{f"in_{n}": a for n, a in arrays.items()}], core_ids=[0])
    y = np.asarray(r.results[0]["out"])
    return y.transpose(1, 0, 2).reshape(1, T, D)
```

```python
from contextlib import ExitStack

import concourse.bass as bass
import numpy as np
from concourse import mybir

F32 = mybir.dt.float32
F32R = mybir.dt.float32r
BF16 = mybir.dt.bfloat16
ALU = mybir.AluOpType
ACT = mybir.ActivationFunctionType
AX = mybir.AxisListType

P = 128
T = 2048
D = 256
DK = D // P
NT = T // P
CH = 512
NC = T // CH
TPC = CH // P
EPS = 1e-5
NEG = -1e38

HA, HDA = 16, 16
SCALE_A = 1.0 / float(np.sqrt(HDA))
HPT = P // HDA
UA = 2 * D // P
HB, KVB, HDB = 16, 4, 128
SCALE_B = 1.0 / float(np.sqrt(HDB))
REP = HB // KVB
NE, TOPK, FF = 8, 2, 896
FT = FF // P

QUADS = [(i, q) for i in range(NC) for q in range(i + 1)]
PAIRS = 2 * len(QUADS)
PIECES = [(i, c, min(CH, (i + 1) * P - c * CH)) for i in range(NT) for c in range(i // TPC + 1)]



def wait_apart(eng, sem, value, passed):
    eng.wait_ge(sem, value + 1)
    eng.sem_inc(passed, 1)


class Chain:

    def __init__(self, eng, sem, passed, base=0):
        self.eng, self.sem, self.passed, self.base, self.n = eng, sem, passed, base, 0

    def link(self, ins):
        ins.then_inc(self.sem, 1)
        self.n += 1
        wait_apart(self.eng, self.sem, self.base + self.n, self.passed)


class Core:

    def __init__(self, nc, root):
        self.nc, self.root = nc, root
        self.closed = []
        self.passed = self.sem("passed")

    def sem(self, name, plain=False):
        s = self.root.enter_context(self.nc.semaphore(name))
        if not plain:
            self.closed.append(s)
        return s

    def open_semaphores(self, eng):
        for s in self.closed:
            eng.sem_inc(s, 1)
        self.closed = []

    def keep(self, name, shape, dt=F32):
        return self.root.enter_context(self.nc.sbuf_tensor(name, shape, dt))

    def scratch(self, name, shape, dt=F32):
        return self.nc.dram_tensor(name, shape, dt, kind="Internal").ap()


def phase_sbuf(nc, stack):
    def sb(name, shape, dt=F32):
        return stack.enter_context(nc.sbuf_tensor(name, shape, dt))
    return sb


def raw(ap):
    return ap.bitcast(F32)


def three_products(nc, out, w_hi, w_lo, x_hi, x_lo, first, last):
    nc.tensor.matmul(out, w_hi, x_hi, start=first, stop=False, skip_group_check=True)
    nc.tensor.matmul(out, w_lo, x_hi, start=False, stop=False, skip_group_check=True)
    return nc.tensor.matmul(out, w_hi, x_lo, start=False, stop=last, skip_group_check=True)



def root(core, act, out, var, asked, asked_at, answered):
    act.wait_ge(asked, asked_at + 1)
    core.nc.scalar.activation(out, var, ACT.Sqrt, bias=core.eps[:]).then_inc(answered, 1)


def layer_norm_stats(nc, chain, core, src, answered, answer):
    for t in range(TPC):
        last = nc.vector.bn_stats(core.stats[:, t, :], src(t))
    chain.link(last)
    for t in range(TPC):
        last = nc.vector.bn_aggr(core.mv[:, t, :], core.stats[:, t, :])
    chain.link(last)
    chain.eng.wait_ge(answered, answer + 1)
    chain.link(nc.vector.reciprocal(core.rstd[:], core.rstd[:]))


def rms_norm_stats(nc, chain, core, src, answered, answer):
    for t in range(TPC):
        last = nc.vector.bn_stats(core.stats[:, t, :], src(t))
    chain.link(last)
    for t in range(TPC):
        last = nc.vector.bn_aggr(core.mv[:, t, :], core.stats[:, t, :])
    chain.link(last)
    chain.link(nc.vector.tensor_tensor(core.rstd[:, :, :], core.mv[:, :, 0:1], core.mv[:, :, 0:1], ALU.mult))
    chain.link(nc.vector.tensor_tensor(core.rstd[:, :, :], core.rstd[:, :, :], core.mv[:, :, 1:2], ALU.add))
    chain.eng.wait_ge(answered, answer + 1)
    chain.link(nc.vector.reciprocal(core.rstd[:], core.rstd[:]))


def phase_norm(core, tag, mode, hT, gate=None, load=None):
    nc = core.nc
    hT_hi, hT_lo = hT
    which = {"ln": 0, "ln_rms": 1, "rms": 2}[mode]
    with ExitStack() as st:
        sb = phase_sbuf(nc, st)
        xn = sb(f"xn_{tag}", [P, TPC, D])
        hf = sb(f"hf_{tag}", [P, DK, CH])
        tr = st.enter_context(nc.psum_tensor(f"tr_{tag}", [P, DK, CH], F32))
        pl = st.enter_context(nc.psum_tensor(f"pl_{tag}", [P, CH], F32))
        loaded = core.sem(f"loaded_{tag}")
        normed = core.sem(f"normed_{tag}")
        transposed = core.sem(f"transposed_{tag}")
        hi_done = core.sem(f"hi_done_{tag}")
        lo_done = core.sem(f"lo_done_{tag}")
        chained = core.sem(f"chained_{tag}")
        hf_done = core.sem(f"hf_done_{tag}")
        routed = core.sem(f"routed_{tag}")
        rooted = core.sem(f"rooted_{tag}")
        logits_out = core.sem(f"logits_out_{tag}")
        with nc.Block() as block:
            @block.sync
            def _(sp):
                core.open_semaphores(sp)
                if load:
                    load(sp, loaded)

            n_loads = load.count if load else 0
            CHAIN = {"ln": 4, "ln_rms": 10, "rms": 6}[mode]
            ROOTS = {"ln": 1, "ln_rms": 2, "rms": 1}[mode]

            @block.vector
            def _(dve):
                if load:
                    dve.wait_ge(loaded, 16 * n_loads + 1)
                    nc.vector.memset(core.ones[:], 1.0)
                    nc.vector.memset(core.eps[:], EPS)
                def normalise(c):
                    chain = Chain(dve, chained, core.passed, c * CHAIN)
                    src = core.R if mode == "rms" else core.X
                    tile = lambda t: src[:, bass.ds(c * TPC + t, 1), :].rearrange("p a d -> p (a d)")
                    if mode != "rms":
                        layer_norm_stats(nc, chain, core, tile, rooted, c * ROOTS + 1)
                    dve.wait_ge(transposed, c + 1)
                    if mode == "ln":
                        for t in range(TPC):
                            last = nc.vector.tensor_scalar(xn[:, t, :], tile(t), core.mv[:, t, 0:1],
                                                           core.rstd[:, t, :], ALU.subtract, ALU.mult)
                        chain.link(last)
                        last_done = None
                    else:
                        if mode == "ln_rms":
                            for t in range(TPC):
                                rt = core.R[:, bass.ds(c * TPC + t, 1), :].rearrange("p a d -> p (a d)")
                                last = nc.vector.tensor_scalar(rt, tile(t), core.mv[:, t, 0:1],
                                                               core.rstd[:, t, :], ALU.subtract, ALU.mult)
                            chain.link(last)
                        rtile = lambda t: core.R[:, bass.ds(c * TPC + t, 1), :].rearrange("p a d -> p (a d)")
                        rms_norm_stats(nc, chain, core, rtile, rooted, (c + 1) * ROOTS)
                        for t in range(TPC):
                            last = nc.vector.tensor_scalar(xn[:, t, :], rtile(t), core.rstd[:, t, :], None, ALU.mult)
                        chain.link(last)
                    assert chain.n == CHAIN, chain.n

                def low_part(c):
                    for dk in range(DK):
                        dve.wait_ge(hi_done, c * DK + dk + 2)
                        lo = nc.vector.scalar_tensor_tensor(
                            hT_lo[:, dk, bass.ds(c * CH, CH)], tr[:, dk, :], core.wcol[:, which, dk:dk + 1],
                            hT_hi[:, dk, bass.ds(c * CH, CH)], ALU.mult, ALU.subtract)
                        lo.then_inc(lo_done, 1)

                def take_logits(c):
                    dve.wait_ge(routed, c + 2)
                    nc.vector.tensor_copy(
                        core.logits[:, bass.ds(c * TPC, TPC), :],
                        pl[:, 0:TPC * NE].rearrange("p (t e) -> p t e", e=NE)).then_inc(logits_out, 1)

                normalise(0)
                normalise(1)
                low_part(0)
                with dve.Fori(1, NC - 1) as c:
                    normalise(c + 1)
                    if gate is not None:
                        take_logits(c - 1)
                    low_part(c)
                if gate is not None:
                    take_logits(NC - 2)
                low_part(NC - 1)
                if gate is not None:
                    take_logits(NC - 1)

            @block.tensor
            def _(pe):
                with pe.Fori(0, NC) as c:
                    pe.wait_ge(chained, (c + 1) * CHAIN + 1)
                    pe.wait_ge(lo_done, c * DK + 1)
                    if gate is not None:
                        pe.wait_ge(hf_done, c * DK + 1)
                    for dk in range(DK):
                        for t in range(TPC):
                            last = nc.tensor.transpose(tr[:, dk, t * P:(t + 1) * P],
                                                       xn[:, t, dk * P:(dk + 1) * P], core.ident[:])
                    last.then_inc(transposed, 1)
                    if gate is not None:
                        pe.wait_ge(hf_done, (c + 1) * DK + 1)
                        pe.wait_ge(logits_out, c + 1)
                        for t in range(TPC):
                            for dk in range(DK):
                                last = nc.tensor.matmul(pl[:, t * NE:(t + 1) * NE], hf[:, dk, t * P:(t + 1) * P],
                                                        gate[:, dk, :], start=(dk == 0), stop=(dk == DK - 1))
                        last.then_inc(routed, 1)

            @block.scalar
            def _(act):
                def roots(c):
                    if mode != "rms":
                        root(core, act, core.rstd[:], core.mv[:, :, 1:2], chained, c * CHAIN + 2, rooted)
                    if mode != "ln":
                        root(core, act, core.rstd[:], core.rstd[:], chained, (c + 1) * CHAIN - 2, rooted)

                def high_part(c):
                    act.wait_ge(transposed, c + 2)
                    for dk in range(DK):
                        nc.scalar.activation(hT_hi[:, dk, bass.ds(c * CH, CH)], tr[:, dk, :], ACT.Copy,
                                             scale=core.wcol[:, which, dk:dk + 1]).then_inc(hi_done, 1)
                    if gate is not None:
                        act.wait_ge(routed, c + 1)
                        for dk in range(DK):
                            act.wait_ge(lo_done, c * DK + dk + 2)
                            nc.scalar.activation(hf[:, dk, :], tr[:, dk, :], ACT.Copy,
                                                 scale=core.wcol[:, which, dk:dk + 1]).then_inc(hf_done, 1)

                roots(0)
                with act.Fori(0, NC - 1) as c:
                    roots(c + 1)
                    high_part(c)
                high_part(NC - 1)


def phase_project_a(core, hT, V_all, wa_in, cos_in, sin_in):
    nc = core.nc
    hT_hi, hT_lo = hT
    NQK, NW = 2 * D, 5 * D
    with ExitStack() as st:
        sb = phase_sbuf(nc, st)
        w_raw = sb("wa_raw", [P, DK, NW])
        w_hi = sb("wa_hi", [P, DK, NW], F32R)
        w_lo = sb("wa_lo", [P, DK, NW], F32R)
        cos = sb("cos_a", [P, T])
        sin = sb("sin_a", [P, T])
        rot = sb("rot_a", [P, 3, CH])
        r_hi = sb("r_hi_a", [P, 2, CH], F32R)
        r_lo = sb("r_lo_a", [P, 2, CH], F32R)
        ps = st.enter_context(nc.psum_tensor("ps_pa", [P, 2, 2, CH], F32))
        pv = st.enter_context(nc.psum_tensor("pv_pa", [P, 2, CH], F32))
        w_loaded, w_split, w_high = core.sem("wa_loaded"), core.sem("wa_split"), core.sem("wa_high")
        projected, rotated, chained = core.sem("pa_projected"), core.sem("pa_rotated"), core.sem("pa_chained")
        hi_done, lo_done = core.sem("pa_hi"), core.sem("pa_lo")
        stored = [core.sem(f"pa_stored{i}") for i in range(2)]
        v_done, v_out = core.sem("pa_v_done"), core.sem("pa_v_out")
        UNITS = UA * NC
        with nc.Block() as block:
            @block.sync
            def _(sp):
                core.open_semaphores(sp)
                sp.dma_start(w_raw[:], wa_in).then_inc(w_loaded, 16)
                sp.dma_start(cos[:], cos_in).then_inc(w_loaded, 16)
                sp.dma_start(sin[:], sin_in).then_inc(w_loaded, 16)
                with sp.Fori(0, NC) as c:
                    for u in range(UA):
                        for part, buf, done in ((0, r_hi, hi_done), (1, r_lo, lo_done)):
                            sp.wait_ge(done, c * UA + u + 2)
                            dst = core.qk_a[u * HPT:(u + 1) * HPT, part, :, bass.ds(c * CH, CH)]
                            sp.dma_start(dst, raw(buf[:, u % 2, :])).then_inc(stored[u % 2], 16)
                for i in range(2):
                    sp.wait_ge(stored[i], UNITS // 2 * 32 + 1)

            @block.tensor
            def _(pe):
                pe.wait_ge(w_split, 2)
                with pe.Fori(0, NC) as c:
                    for u in range(UA):
                        if u >= 2:
                            pe.wait_ge(rotated, c * UA + u)
                        else:
                            pe.wait_ge(rotated, c * UA + 1)
                        for swap in range(2):
                            o = u * P + swap * 3 * D
                            for dk in range(DK):
                                last = three_products(
                                    nc, ps[:, u % 2, swap, :], w_hi[:, dk, o:o + P], w_lo[:, dk, o:o + P],
                                    hT_hi[:, dk, bass.ds(c * CH, CH)], hT_lo[:, dk, bass.ds(c * CH, CH)],
                                    dk == 0, dk == DK - 1)
                        last.then_inc(projected, 1)
                for t in range(NT):
                    if t >= 2:
                        pe.wait_ge(v_out, t)
                    for dk in range(DK):
                        last = three_products(nc, pv[:, t % 2, 0:D],
                                              hT_hi[:, dk, t * P:(t + 1) * P], hT_lo[:, dk, t * P:(t + 1) * P],
                                              w_hi[:, dk, NQK:NQK + D], w_lo[:, dk, NQK:NQK + D],
                                              dk == 0, dk == DK - 1)
                    last.then_inc(v_done, 1)

            @block.vector
            def _(dve):
                dve.wait_ge(w_high, 2)
                nc.vector.tensor_tensor(w_lo[:], w_raw[:], w_hi[:], ALU.subtract).then_inc(w_split, 1)
                with dve.Fori(0, NC) as c:
                    chain = Chain(dve, chained, core.passed, c * UA)
                    for u in range(UA):
                        dve.wait_ge(projected, c * UA + u + 2)
                        dve.wait_ge(hi_done, c * UA + u + 1)
                        nc.vector.tensor_tensor(rot[:, 0, :], ps[:, u % 2, 0, :], cos[:, bass.ds(c * CH, CH)], ALU.mult)
                        chain.link(nc.vector.tensor_tensor(rot[:, 1, :], ps[:, u % 2, 1, :],
                                                           sin[:, bass.ds(c * CH, CH)], ALU.mult))
                        nc.vector.tensor_tensor(rot[:, 2, :], rot[:, 0, :], rot[:, 1, :], ALU.add).then_inc(rotated, 1)
                        dve.wait_ge(hi_done, c * UA + u + 2)
                        nc.vector.tensor_tensor(r_lo[:, u % 2, :], rot[:, 2, :], r_hi[:, u % 2, :],
                                                ALU.subtract).then_inc(lo_done, 1)

            @block.scalar
            def _(act):
                act.wait_ge(w_loaded, 49)
                nc.scalar.activation(w_hi[:], w_raw[:], ACT.Copy).then_inc(w_high, 1)
                with act.Fori(0, NC) as c:
                    for u in range(UA):
                        act.wait_ge(rotated, c * UA + u + 2)
                        if u >= 2:
                            act.wait_ge(stored[u % 2], c * (UA // 2 * 32) + 32 + 1)
                        else:
                            act.wait_ge(stored[u % 2], c * (UA // 2 * 32) + 1)
                        nc.scalar.activation(r_hi[:, u % 2, :], rot[:, 2, :], ACT.Copy).then_inc(hi_done, 1)
                for t in range(NT):
                    act.wait_ge(v_done, t + 2)
                    nc.scalar.activation(V_all[:, t, :], pv[:, t % 2, 0:D], ACT.Copy).then_inc(v_out, 1)


def phase_attention_a(core, V_all, O_all):
    nc = core.nc
    SR = 4 * HDA
    VW = 32
    NB = 3
    SLOW = len(QUADS) - 2
    PPQ = len(PIECES) // SLOW
    assert PPQ * SLOW == len(PIECES)
    NQ, NPC = len(QUADS), len(PIECES)
    ends = {QUADS.index((i, i)): i for i in range(NC)}
    with ExitStack() as st:
        sb = phase_sbuf(nc, st)
        Q = [sb(f"Qst{i}", [P, T], F32R) for i in range(NB)]
        K = [sb(f"Kst{i}", [P, T], F32R) for i in range(NB)]
        V = [sb(f"Vh{i}", [P, NT, VW]) for i in range(NB)]
        p = sb("p_a", [P, 4, 2, CH])
        oT = sb("oT_a", [P, CH])
        mxp = sb("mxp_a", [P, NT, NC])
        nm = sb("nm_a", [P, NT])
        nmT_hi = sb("nmT_hi_a", [NT, P], F32R)
        nmT_lo = sb("nmT_lo_a", [NT, P], F32R)
        osum = sb("osum_a", [P, TPC, HDA + 1])
        orec = sb("orec_a", [P, TPC, 1])
        ps = st.enter_context(nc.psum_tensor("ps_aa", [P, 2, 2, CH], F32))
        pm = st.enter_context(nc.psum_tensor("pm_aa", [P, 2, CH], F32))
        po = st.enter_context(nc.psum_tensor("po_aa", [P, CH], F32))
        pt = st.enter_context(nc.psum_tensor("pt_aa", [P, CH], F32))
        qk_loaded = [core.sem(f"aa_qk_loaded{i}") for i in range(NB)]
        max_loaded = [core.sem(f"aa_max_loaded{i}") for i in range(NB)]
        k_padded, q_padded, v_ready = core.sem("aa_k_padded"), core.sem("aa_q_padded"), core.sem("aa_v_ready")
        v_padded, m_padded = core.sem("aa_v_padded"), core.sem("aa_m_padded")
        piece_done, piece_max, max_ready = core.sem("aa_piece_done"), core.sem("aa_piece_max"), core.sem("aa_max_ready")
        max_T, max_hi, max_lo = core.sem("aa_max_T"), core.sem("aa_max_hi"), core.sem("aa_max_lo")
        scored, exped, valued = core.sem("aa_scored"), core.sem("aa_exped"), core.sem("aa_valued")
        o_copied, o_T, o_summed, o_done = core.sem("aa_o_copied"), core.sem("aa_o_T"), core.sem("aa_o_summed"), core.sem("aa_o_done")
        chained = core.sem("aa_chained")

        def steps(eng, step, peel=0):
            def three(j):
                step((NB * j, 0, j), (NB * j + 1, 1, j))
                step((NB * j + 1, 1, j), (NB * j + 2, 2, j))
                step((NB * j + 2, 2, j), (NB * j + 3, 0, j + 1))
            step(None, (0, 0, 0))
            turns = (HA - 1) // NB
            with eng.Fori(0, turns - peel) as j:
                three(j)
            if peel:
                three(turns - 1)
            step((HA - 1, 0, turns), None)
        assert (HA - 1) % NB == 0

        def wait(eng, s, value):
            if not isinstance(value, int) or value > 0:
                eng.wait_ge(s, value + 1)

        with nc.Block() as block:
            @block.sync
            def _(sp):
                core.open_semaphores(sp)
                def load(head, par):
                    wait(sp, scored, (head - 2) * PAIRS)
                    for part in range(2):
                        src = core.qk_a[bass.ds(head, 1), part, :, :].rearrange("a r t -> (a r) t")
                        for rep in range(2):
                            r0 = (2 * part + rep) * HDA
                            sp.dma_start(raw(Q[par][r0:r0 + HDA, :]), src).then_inc(qk_loaded[par], 16)
                        src = core.qk_a[bass.ds(head + HA, 1), part, :, :].rearrange("a r t -> (a r) t")
                        for rep in range(2):
                            r0 = (2 * rep + part) * HDA
                            sp.dma_start(raw(K[par][r0:r0 + HDA, :]), src).then_inc(qk_loaded[par], 16)

                def step(t, m):
                    if m is not None:
                        h, par, use = m
                        if t is not None and not (isinstance(h, int) and h == HA - 1):
                            load(h + 1, (par + 1) % NB)
                        sp.wait_ge(max_hi, h + 2)
                        sp.dma_start(raw(Q[par][SR:SR + 1, :]), raw(nmT_hi[:])).then_inc(max_loaded[par], 16)
                        sp.wait_ge(max_lo, h + 2)
                        sp.dma_start(raw(Q[par][SR + 1:SR + 2, :]), raw(nmT_lo[:])).then_inc(max_loaded[par], 16)
                load(0, 0)
                load(1, 1)
                steps(sp, step, peel=1)

            @block.gpsimd
            def _(pool):
                def step(t, m):
                    if m is not None:
                        h, par, use = m
                        if not isinstance(h, int):
                            before = NB * use if par == 2 else h - 2 if par == 0 else NB * use
                            wait_apart(pool, valued, before * NQ, core.passed)
                        nc.gpsimd.memset(raw(Q[par][SR:SR + 2, :]), 0.0).then_inc(q_padded, 1)
                        pool.wait_ge(q_padded, h + 2)
                        src = V_all[:, :, bass.ds(h * HDA, HDA)]
                        nc.gpsimd.tensor_copy(V[par][:, :, 0:HDA], src).then_inc(v_ready, 1)
                        pool.wait_ge(v_ready, h + 2)
                pool.wait_ge(k_padded, 3 * NB + 1)
                pool.wait_ge(v_padded, 2 * NB + 1)
                steps(pool, step)

            @block.tensor
            def _(pe):
                pe.wait_ge(k_padded, 3 * NB + 1)

                def step(t, m):
                    if t is not None:
                        th, tp, tu = t
                    if m is not None:
                        mh, mp, mu = m
                        pe.wait_ge(qk_loaded[mp], (mu + 1) * 128 + 1)
                        pe.wait_ge(q_padded, mh + 2)
                        wait(pe, max_lo, mh)

                    def piece(k):
                        i, c, w = PIECES[k]
                        wait(pe, piece_max, mh * NPC + k - 1)
                        diag = c == i // TPC
                        out = pm[:, k % 2, 0:w]
                        last = nc.tensor.matmul(out, Q[mp][:, i * P:(i + 1) * P], K[mp][:, c * CH:c * CH + w],
                                                start=True, stop=not diag, skip_group_check=True)
                        if diag:
                            last = nc.tensor.matmul(pm[:, k % 2, w - P:w], core.identb[:], core.maskq[:],
                                                    start=False, stop=True, skip_group_check=True)
                        last.then_inc(piece_done, 1)

                    def scores(n, half):
                        i, q = QUADS[n]
                        pair = 2 * n + half
                        pe.wait_ge(exped, th * PAIRS + max(0, pair - 1) + 1)
                        for j in range(2):
                            g = 2 * half + j
                            kt = TPC * q + g
                            out = ps[:, half, j, :]
                            last = nc.tensor.matmul(out, K[tp][:, kt * P:(kt + 1) * P], Q[tp][:, i * CH:(i + 1) * CH],
                                                    start=True, stop=q < i, skip_group_check=True)
                            if q == i:
                                w = (g + 1) * P
                                last = nc.tensor.matmul(ps[:, half, j, 0:w], core.identb[:],
                                                        core.maskt[:, 3 * P - g * P:3 * P - g * P + w],
                                                        start=False, stop=True, skip_group_check=True)
                        last.then_inc(scored, 1)

                    def values(n):
                        i, q = QUADS[n]
                        pe.wait_ge(exped, th * PAIRS + 2 * n + 2 + 1)
                        if q == 0:
                            wait(pe, o_copied, th * NC + i)
                        for g in range(TPC):
                            pair = 2 * n + g // 2
                            last = nc.tensor.matmul(po[g * VW:(g + 1) * VW, :], V[tp][:, TPC * q + g, :],
                                                    p[:, pair % 4, g % 2, :], start=(q == 0), stop=(q == i),
                                                    skip_group_check=True)
                        last.then_inc(valued, 1)

                    def turn(i):
                        pe.wait_ge(o_copied, th * NC + i + 2)
                        wait(pe, o_summed, th * NC + i)
                        for r in range(TPC):
                            last = nc.tensor.transpose(pt[:, r * P:(r + 1) * P], oT[:, r * P:(r + 1) * P], core.ident[:])
                        last.then_inc(o_T, 1)

                    if t is not None:
                        pe.wait_ge(max_loaded[tp], (tu + 1) * 32 + 1)
                        pe.wait_ge(v_ready, th + 2)
                    k = 0
                    for n in range(NQ):
                        for half in range(2):
                            if t is not None:
                                scores(n, half)
                            if m is not None and n < SLOW:
                                for _ in range(2):
                                    piece(k)
                                    k += 1
                        if t is not None and n >= 1:
                            values(n - 1)
                        if m is not None and n < SLOW:
                            piece(k)
                            k += 1
                        if t is not None and n - 2 in ends:
                            turn(ends[n - 2])
                        if m is not None and n == SLOW:
                            pe.wait_ge(max_ready, mh + 2)
                            nc.tensor.transpose(pm[0:NT, 0, 0:P], nm[:, :], core.ident[:]).then_inc(max_T, 1)
                    if t is not None:
                        values(NQ - 1)
                        turn(NC - 1)
                steps(pe, step)

            @block.scalar
            def _(act):
                def step(t, m):
                    def copy_out(i):
                        act.wait_ge(valued, (t[0] * NQ + [n for n in ends if ends[n] == i][0] + 1) + 1)
                        wait(act, o_T, t[0] * NC + i)
                        nc.scalar.activation(oT[:], po[:], ACT.Copy).then_inc(o_copied, 1)

                    for n in range(NQ):
                        if t is not None:
                            th = t[0]
                            for half in range(2):
                                pair = 2 * n + half
                                act.wait_ge(scored, th * PAIRS + pair + 2)
                                wait(act, valued, th * NQ + n - 1 if n >= 1 else th * NQ)
                                nc.scalar.activation(p[:, pair % 4, :, :], ps[:, half, :, :], ACT.Exp,
                                                     scale=SCALE_A).then_inc(exped, 1)
                            if n - 1 in ends:
                                copy_out(ends[n - 1])
                        if m is not None and n == SLOW:
                            act.wait_ge(max_T, m[0] + 2)
                            prev, uses = (m[1] - 1) % NB, m[2] + (m[1] > 0)
                            wait(act, max_loaded[prev], uses * 32)
                            nc.scalar.activation(nmT_hi[:], pm[0:NT, 0, 0:P], ACT.Copy).then_inc(max_hi, 1)
                    if t is not None:
                        copy_out(NC - 1)
                steps(act, step)

            @block.vector
            def _(dve):
                for i in range(NB):
                    nc.vector.memset(raw(K[i][SR:P, :]), 0.0).then_inc(k_padded, 1)
                    nc.vector.memset(raw(Q[i][SR:P, :]), 0.0).then_inc(k_padded, 1)
                    nc.vector.memset(V[i][:], 0.0).then_inc(v_padded, 1)
                nc.vector.memset(mxp[:], 3e38).then_inc(m_padded, 1)
                dve.wait_ge(m_padded, 2)
                dve.wait_ge(k_padded, 2 * NB + 1)
                dve.wait_ge(v_padded, NB + 1)
                for i in range(NB):
                    nc.vector.memset(raw(K[i][SR:SR + 2, :]), 1.0).then_inc(k_padded, 1)
                    nc.vector.memset(V[i][:, :, HDA:HDA + 1], 1.0).then_inc(v_padded, 1)

                def step(t, m):
                    def finish(i):
                        th = t[0]
                        dve.wait_ge(o_T, th * NC + i + 2)
                        wait(dve, o_done, th * NC + i)
                        src = pt[:, :].rearrange("p (t g v) -> p t v g", t=TPC, v=VW)[:, :, 0:HDA + 1, :]
                        nc.vector.tensor_reduce(osum[:], src, axis=AX.X, op=ALU.add).then_inc(o_summed, 1)
                        dve.wait_ge(o_summed, th * NC + i + 2)
                        nc.vector.reciprocal(orec[:], osum[:, :, HDA:HDA + 1]).then_inc(chained, 1)
                        dve.wait_ge(chained, th * NC + i + 2)
                        nc.vector.tensor_tensor(O_all[:, i * TPC:(i + 1) * TPC, bass.ds(th * HDA, HDA)],
                                                osum[:, :, 0:HDA], orec[:].broadcast_to([P, TPC, HDA]),
                                                ALU.mult).then_inc(o_done, 1)

                    k = 0
                    for n in range(NQ):
                        if m is not None and n < SLOW:
                            for _ in range(PPQ):
                                i, c, w = PIECES[k]
                                dve.wait_ge(piece_done, m[0] * NPC + k + 2)
                                nc.vector.tensor_reduce(mxp[:, i, c:c + 1], pm[:, k % 2, 0:w], axis=AX.X,
                                                        op=ALU.max, negate=True).then_inc(piece_max, 1)
                                k += 1
                        if m is not None and n == SLOW - 1:
                            dve.wait_ge(piece_max, (m[0] + 1) * NPC + 1)
                            nc.vector.tensor_reduce(nm[:], mxp[:], axis=AX.X, op=ALU.min).then_inc(max_ready, 1)
                        if t is not None and n - 2 in ends:
                            finish(ends[n - 2])
                        if m is not None and n == SLOW:
                            dve.wait_ge(max_hi, m[0] + 2)
                            nc.vector.tensor_tensor(nmT_lo[:], pm[0:NT, 0, 0:P], nmT_hi[:],
                                                    ALU.subtract).then_inc(max_lo, 1)
                    if t is not None:
                        finish(NC - 1)
                steps(dve, step)


def phase_output_a(core, O_all, woa_in):
    nc = core.nc
    with ExitStack() as st:
        sb = phase_sbuf(nc, st)
        wo = sb("woa", [P, DK, D])
        wo_hi = sb("woa_hi", [P, DK, D], F32R)
        wo_lo = sb("woa_lo", [P, DK, D], F32R)
        ot_hi = sb("ot_hi_a", [P, 2, DK, P], F32R)
        ot_lo = sb("ot_lo_a", [P, 2, DK, P], F32R)
        stats = sb("stats_oa", [P, 6])
        mv = sb("mv_oa", [P, 2])
        rs = sb("rs_oa", [P, 1])
        yn = sb("yn_oa", [P, D])
        pt = st.enter_context(nc.psum_tensor("pt_oa", [P, 2, CH], F32))
        py = st.enter_context(nc.psum_tensor("py_oa", [P, 2, CH], F32))
        w_loaded, w_high, w_split = core.sem("oa_w_loaded"), core.sem("oa_w_high"), core.sem("oa_w_split")
        turned, hi_done, lo_done = core.sem("oa_turned"), core.sem("oa_hi"), core.sem("oa_lo")
        y_done, y_out, chained = core.sem("oa_y_done"), core.sem("oa_y_out"), core.sem("oa_chained")
        rooted = core.sem("oa_rooted")
        with nc.Block() as block:
            @block.sync
            def _(sp):
                core.open_semaphores(sp)
                sp.dma_start(wo[:], woa_in).then_inc(w_loaded, 16)

            @block.tensor
            def _(pe):
                def turn(t):
                    if t >= 2:
                        pe.wait_ge(lo_done, t)
                    for dk in range(DK):
                        last = nc.tensor.transpose(pt[:, t % 2, dk * P:(dk + 1) * P],
                                                   O_all[:, t, dk * P:(dk + 1) * P], core.ident[:])
                    last.then_inc(turned, 1)
                turn(0)
                for t in range(NT):
                    if t + 1 < NT:
                        turn(t + 1)
                    if t == 0:
                        pe.wait_ge(w_split, 2)
                    pe.wait_ge(lo_done, t + 2)
                    if t >= 2:
                        pe.wait_ge(y_out, t)
                    for dk in range(DK):
                        last = three_products(nc, py[:, t % 2, 0:D], ot_hi[:, t % 2, dk, :], ot_lo[:, t % 2, dk, :],
                                              wo_hi[:, dk, :], wo_lo[:, dk, :], dk == 0, dk == DK - 1)
                    last.then_inc(y_done, 1)

            @block.scalar
            def _(act):
                act.wait_ge(w_loaded, 17)
                nc.scalar.activation(wo_hi[:], wo[:], ACT.Copy).then_inc(w_high, 1)

                def high(t):
                    act.wait_ge(turned, t + 2)
                    if t >= 2:
                        act.wait_ge(y_done, t)
                    nc.scalar.activation(ot_hi[:, t % 2, :, :], pt[:, t % 2, 0:D].rearrange("p (k t) -> p k t", k=DK),
                                         ACT.Copy).then_inc(hi_done, 1)
                high(0)
                for t in range(NT):
                    if t + 1 < NT:
                        high(t + 1)
                    root(core, act, rs[:], mv[:, 1:2], chained, 4 * t + 2, rooted)

            @block.vector
            def _(dve):
                dve.wait_ge(w_high, 2)
                nc.vector.tensor_tensor(wo_lo[:], wo[:], wo_hi[:], ALU.subtract).then_inc(w_split, 1)
                chain = Chain(dve, chained, core.passed)

                def low(t):
                    dve.wait_ge(hi_done, t + 2)
                    nc.vector.tensor_tensor(ot_lo[:, t % 2, :, :],
                                            pt[:, t % 2, 0:D].rearrange("p (k t) -> p k t", k=DK),
                                            ot_hi[:, t % 2, :, :], ALU.subtract).then_inc(lo_done, 1)
                low(0)
                for t in range(NT):
                    if t + 1 < NT:
                        low(t + 1)
                    dve.wait_ge(y_done, t + 2)
                    y = py[:, t % 2, 0:D]
                    chain.link(nc.vector.bn_stats(stats[:], y))
                    chain.link(nc.vector.bn_aggr(mv[:], stats[:]))
                    dve.wait_ge(rooted, t + 2)
                    chain.link(nc.vector.reciprocal(rs[:], rs[:]))
                    ins = nc.vector.tensor_scalar(yn[:], y, mv[:, 0:1], rs[:], ALU.subtract, ALU.mult)
                    ins.then_inc(y_out, 1)
                    dve.wait_ge(y_out, t + 2)
                    chain.link(nc.vector.tensor_tensor(core.X[:, t, :], core.X[:, t, :], yn[:], ALU.add))


def phase_project_b(core, hT, wq_in, wkv_in, cos_in, sin_in):
    nc = core.nc
    hT_hi, hT_lo = hT
    NH = HB + KVB
    HALF = P // 2
    RB, WB = 4, 4
    assert NH % RB == 0
    NWC = (HB + 2 * KVB) * HDB

    def stores_before(h):
        return sum(2 if k in (HB - 1, NH - 1) else 1 for k in range(h % RB, h, RB))
    STORES = [stores_before(NH + i) for i in range(RB)]
    with ExitStack() as st:
        sb = phase_sbuf(nc, st)
        w_raw = sb("wb_raw", [P, WB, 4, P])
        w_hi = sb("wb_hi", [P, DK, NWC], F32R)
        w_lo = sb("wb_lo", [P, DK, NWC], F32R)
        cos = sb("cos_b", [P, T])
        sin = sb("sin_b", [P, T])
        sw = sb("sw_b", [P, 2, CH])
        tc = sb("tc_b", [P, 2, CH])
        ts = sb("ts_b", [P, 2, CH])
        r = sb("r_b", [P, RB, CH])
        v_hi = sb("v_hi_b", [P, 2, KVB * HDB], F32R)
        v_lo = sb("v_lo_b", [P, 2, KVB * HDB], F32R)
        ps = st.enter_context(nc.psum_tensor("ps_pb", [P, 4, CH], F32))
        loaded = [core.sem(f"pb_loaded{i}") for i in range(WB)]
        tab_loaded = core.sem("pb_tab")
        w_high, w_low = core.sem("pb_w_high"), core.sem("pb_w_low")
        projected, cos_done, swapped = core.sem("pb_projected"), core.sem("pb_cos_done"), core.sem("pb_swapped")
        sin_done, r_done = core.sem("pb_sin_done"), core.sem("pb_r_done")
        stored = [core.sem(f"pb_stored{i}") for i in range(RB)]
        v_done, v_high, v_low = core.sem("pb_v_done"), core.sem("pb_v_high"), core.sem("pb_v_low")
        v_stored = [core.sem(f"pb_v_stored{i}") for i in range(2)]
        WT = NWC // CH
        pieces = [(dk, w) for dk in range(DK) for w in range(WT)]
        with nc.Block() as block:
            @block.sync
            def _(sp):
                core.open_semaphores(sp)
                for n, (dk, w) in enumerate(pieces):
                    if n == WB:
                        sp.dma_start(cos[:], cos_in).then_inc(tab_loaded, 16)
                        sp.dma_start(sin[:], sin_in).then_inc(tab_loaded, 16)
                    if n >= WB:
                        sp.wait_ge(w_low, n - WB + 2)
                    sp.dma_start(w_raw[:, n % WB, :, :], wq_in[:, dk, w * 4:(w + 1) * 4, :]).then_inc(loaded[n % WB], 16)
                with sp.Fori(0, NC) as c:
                    for h in range(NH):
                        sp.wait_ge(r_done, c * NH + h + 2)
                        dst = core.q_b[h] if h < HB else core.k_b[h - HB]
                        sp.dma_start(dst[:, bass.ds(c * CH, CH)], r[:, h % RB, :]).then_inc(stored[h % RB], 16)
                        if h in (HB - 1, NH - 1):
                            dst = core.q_b[HB] if h < HB else core.k_b[KVB]
                            sp.dma_start(dst[:, bass.ds(c * CH, CH)], r[:, h % RB, :]).then_inc(stored[h % RB], 16)
                for t in range(NT):
                    for part, buf, done in ((0, v_hi, v_high), (1, v_lo, v_low)):
                        sp.wait_ge(done, t + 2)
                        sp.dma_start(core.v_b[0:KVB, part, :, t, :].rearrange("g p d -> p g d"),
                                     raw(buf[:, t % 2, :]).rearrange("p (g d) -> p g d", g=KVB)).then_inc(v_stored[t % 2], 16)
                        sp.dma_start(core.v_b[KVB, part, :, t, :],
                                     raw(buf[:, t % 2, (KVB - 1) * HDB:])).then_inc(v_stored[t % 2], 16)
                for i in range(RB):
                    sp.wait_ge(stored[i], STORES[i] * NC * 16 + 1)
                for i in range(2):
                    sp.wait_ge(v_stored[i], NT // 2 * 64 + 1)

            @block.tensor
            def _(pe):
                pe.wait_ge(w_low, len(pieces) + 1)
                with pe.Fori(0, NC) as c:
                    for h in range(NH):
                        if h >= 4:
                            pe.wait_ge(cos_done, c * NH + h - 3 + 1)
                            pe.wait_ge(swapped, c * NH + h - 3 + 1)
                        else:
                            pe.wait_ge(cos_done, c * NH + 1)
                            pe.wait_ge(swapped, c * NH + 1)
                        for dk in range(DK):
                            last = three_products(
                                nc, ps[:, h % 4, :], w_hi[:, dk, h * P:(h + 1) * P], w_lo[:, dk, h * P:(h + 1) * P],
                                hT_hi[:, dk, bass.ds(c * CH, CH)], hT_lo[:, dk, bass.ds(c * CH, CH)],
                                dk == 0, dk == DK - 1)
                        last.then_inc(projected, 1)
                pe.wait_ge(cos_done, NC * NH + 1)
                pe.wait_ge(swapped, NC * NH + 1)
                for t in range(NT):
                    if t >= 2:
                        pe.wait_ge(v_low, t)
                    for dk in range(DK):
                        last = three_products(nc, ps[:, t % 2, :],
                                              hT_hi[:, dk, t * P:(t + 1) * P], hT_lo[:, dk, t * P:(t + 1) * P],
                                              w_hi[:, dk, NH * P:NWC], w_lo[:, dk, NH * P:NWC],
                                              dk == 0, dk == DK - 1)
                    last.then_inc(v_done, 1)

            @block.scalar
            def _(act):
                for n, (dk, w) in enumerate(pieces):
                    act.wait_ge(loaded[n % WB], (n // WB + 1) * 16 + 1)
                    nc.scalar.activation(w_hi[:, dk, w * CH:(w + 1) * CH],
                                         w_raw[:, n % WB, :, :].rearrange("p a b -> p (a b)"), ACT.Copy).then_inc(w_high, 1)
                with act.Fori(0, NC) as c:
                    for h in range(NH):
                        act.wait_ge(projected, c * NH + h + 2)
                        if h >= 2:
                            act.wait_ge(sin_done, c * NH + h)
                        else:
                            act.wait_ge(sin_done, c * NH + 1)
                        nc.scalar.activation(sw[0:HALF, h % 2, :], ps[HALF:P, h % 4, :], ACT.Copy)
                        nc.scalar.activation(sw[HALF:P, h % 2, :], ps[0:HALF, h % 4, :], ACT.Copy).then_inc(swapped, 1)
                for t in range(NT):
                    act.wait_ge(v_done, t + 2)
                    if t >= 2:
                        act.wait_ge(v_stored[t % 2], (t // 2) * 64 + 1)
                    nc.scalar.activation(v_hi[:, t % 2, :], ps[:, t % 2, :], ACT.Copy).then_inc(v_high, 1)

            @block.gpsimd
            def _(pool):
                pool.wait_ge(tab_loaded, 33)
                with pool.Fori(0, NC) as c:
                    for h in range(NH):
                        if h >= 2:
                            pool.wait_ge(r_done, c * NH + h)
                        else:
                            pool.wait_ge(r_done, c * NH + 1)
                        wait_apart(pool, swapped, c * NH + h + 1, core.passed)
                        nc.gpsimd.tensor_tensor(ts[:, h % 2, :], sw[:, h % 2, :], sin[:, bass.ds(c * CH, CH)],
                                                ALU.mult).then_inc(sin_done, 1)

            @block.vector
            def _(dve):
                for n, (dk, w) in enumerate(pieces):
                    dve.wait_ge(w_high, n + 2)
                    nc.vector.tensor_tensor(w_lo[:, dk, w * CH:(w + 1) * CH],
                                            w_raw[:, n % WB, :, :].rearrange("p a b -> p (a b)"),
                                            w_hi[:, dk, w * CH:(w + 1) * CH], ALU.subtract).then_inc(w_low, 1)
                dve.wait_ge(tab_loaded, 33)
                with dve.Fori(0, NC) as c:
                    def cosine(h):
                        dve.wait_ge(swapped, c * NH + h + 2)
                        nc.vector.tensor_tensor(tc[:, h % 2, :], ps[:, h % 4, :], cos[:, bass.ds(c * CH, CH)],
                                                ALU.mult).then_inc(cos_done, 1)
                    dve.wait_ge(r_done, c * NH + 1)
                    cosine(0)
                    for h in range(NH):
                        if h + 1 < NH:
                            dve.wait_ge(r_done, c * NH + h + 1)
                            cosine(h + 1)
                        dve.wait_ge(sin_done, c * NH + h + 2)
                        dve.wait_ge(cos_done, c * NH + h + 2)
                        dve.wait_ge(stored[h % RB], c * (STORES[h % RB] * 16) + stores_before(h) * 16 + 1)
                        nc.vector.tensor_tensor(r[:, h % RB, :], tc[:, h % 2, :], ts[:, h % 2, :],
                                                ALU.add).then_inc(r_done, 1)
                for t in range(NT):
                    dve.wait_ge(v_high, t + 2)
                    if t >= 2:
                        dve.wait_ge(v_stored[t % 2], (t // 2) * 64 + 1)
                    nc.vector.tensor_tensor(v_lo[:, t % 2, :], ps[:, t % 2, :], v_hi[:, t % 2, :],
                                            ALU.subtract).then_inc(v_low, 1)


def phase_attention_b(core):
    nc = core.nc
    LEAD = 3
    slots = [TPC * (i + 1) + 1 for i in range(NC)]
    slot0 = [sum(slots[:i]) for i in range(NC)]
    SLOTS = sum(slots)
    tiles0 = [TPC * sum(j + 1 for j in range(i)) for i in range(NC)]
    TILES = TPC * sum(j + 1 for j in range(NC))
    parts = [1, 1, 2, 2]
    part0 = [TPC * sum(parts[:i]) for i in range(NC)]
    PARTS = TPC * sum(parts)
    with ExitStack() as st:
        sb = phase_sbuf(nc, st)
        k_raw = sb("k_raw", [P, T])
        k_hi = sb("k_hi", [P, T], F32R)
        k_lo = sb("k_lo", [P, T], F32R)
        v_hi = sb("v_hi", [P, NT, HDB], F32R)
        v_lo = sb("v_lo", [P, NT, HDB], F32R)
        q_raw = sb("q_raw", [P, 2, CH])
        q_hi = sb("q_hi", [P, 2, CH], F32R)
        q_lo = sb("q_lo", [P, 2, CH], F32R)
        p = sb("p_b", [P, 2, TPC, T])
        pT_hi = sb("pT_hi", [P, 3, CH], F32R)
        pT_lo = sb("pT_lo", [P, 3, CH], F32R)
        mx = sb("mx_b", [P, 4, 2])
        bias = sb("bias_b", [P, 2, TPC])
        rsum = sb("rsum_b", [P, 2, TPC])
        rrec = sb("rrec_b", [P, TPC])
        diag = sb("diag_b", [P, TPC, P])
        r_sb = sb("r_sb_b", [P, CH])
        o_sb = sb("o_sb_b", [P, 2, CH])
        ps = st.enter_context(nc.psum_tensor("ps_ab", [P, T], F32))
        pt = st.enter_context(nc.psum_tensor("pt_ab", [P, 3, CH], F32))
        po = st.enter_context(nc.psum_tensor("po_ab", [P, CH], F32))
        k_loaded = core.sem("ab_k_loaded")
        v_loaded = [core.sem(f"ab_v_loaded{i}", plain=True) for i in range(2)]
        q_loaded = [core.sem(f"ab_q_loaded{i}") for i in range(2)]
        k_high, k_low, q_high, q_low = (core.sem(f"ab_{n}") for n in ("k_high", "k_low", "q_high", "q_low"))
        scored, maxed, biased, exped = (core.sem(f"ab_{n}") for n in ("scored", "maxed", "biased", "exped"))
        turned, high, low, valued = (core.sem(f"ab_{n}") for n in ("turned", "high", "low", "valued"))
        inverted, diagonal, spread, spread_out = (core.sem(f"ab_{n}") for n in ("inverted", "diagonal", "spread", "spread_out"))
        o_ready = core.sem("ab_o_ready")
        o_stored = [core.sem(f"ab_o_stored{i}") for i in range(2)]

        def beside(i):
            tiles = TPC * i
            stand = {1: [0, 0, 1, 2], 2: [0, 2, 4, 6], 3: [0, 3, 6, 9], 4: [0, 4, 8, 12]}[i]
            early = 1 if i == 1 else 0
            order = [("row", 0)] * early
            turned_to = 0
            for r in range(TPC):
                while turned_to < min(tiles, stand[r] + LEAD):
                    order.append(("turn", turned_to))
                    turned_to += 1
                if i == NC:
                    order.append(("keys", r))
                if r >= early:
                    order.append(("row", r))
                for k in range(stand[r], stand[r + 1] if r + 1 < TPC else tiles):
                    order.append(("product", k))
                    if turned_to < tiles:
                        order.append(("turn", turned_to))
                        turned_to += 1
            return order

        def heads(eng, head):
            with eng.Fori(0, KVB) as g:
                with eng.Fori(0, REP - 1) as hh:
                    head(g, g * REP + hh, False)
                head(g, g * REP + REP - 1, True)

        with nc.Block() as block:
            @block.sync
            def _(sp):
                core.open_semaphores(sp)

                def load_keys(g):
                    src = core.k_b[bass.ds(g, 1), :, :].rearrange("a p t -> (a p) t")
                    sp.dma_start(k_raw[:], src).then_inc(k_loaded, 16)

                def load_queries(h, i):
                    src = core.q_b[bass.ds(h, 1), :, i * CH:(i + 1) * CH].rearrange("a p t -> (a p) t")
                    sp.dma_start(q_raw[:, i % 2, :], src).then_inc(q_loaded[i % 2], 16)

                def head(g, h, last):
                    for i in range(1, NC):
                        sp.wait_ge(q_low, h * NC + i)
                        load_queries(h, i)
                    if last:
                        sp.wait_ge(k_low, (g + 1) * NC + 1)
                        load_keys(g + 1)
                    sp.wait_ge(q_low, h * NC + NC)
                    load_queries(h + 1, 0)

                load_keys(0)
                load_queries(0, 0)
                heads(sp, head)
                sp.wait_ge(q_low, HB * NC + 1)
                load_queries(HB, 1)
                sp.wait_ge(k_loaded, (KVB + 1) * 16 + 1)
                for i in range(2):
                    sp.wait_ge(q_loaded[i], (HB * NC // 2 + 1) * 16 + 1)
                    sp.wait_ge(o_stored[i], HB * NC // 2 * 16 + 1)

            @block.gpsimd
            def _(pool):
                def load_values(g, half):
                    t0 = half * NT // 2
                    for part, buf in ((0, v_hi), (1, v_lo)):
                        src = core.v_b[bass.ds(g, 1), part, :, t0:t0 + NT // 2, :].rearrange("a p t d -> (a p) t d")
                        pool.dma_start(raw(buf[:, t0:t0 + NT // 2, :]), src).then_inc(v_loaded[half], 16)

                def head(g, h, last):
                    for i in range(NC):
                        if last and i == NC - 1:
                            pool.wait_ge(valued, h * TILES + tiles0[i] + NT // 2 + 1)
                            load_values(g + 1, 0)
                        pool.wait_ge(spread, h * NC + i + 1)
                        wait_apart(pool, inverted, h * NC + i + 1, core.passed)
                        for r in range(TPC):
                            ins = nc.gpsimd.tensor_scalar(diag[:, r, :], core.ident[:], rrec[:, r:r + 1], None, ALU.mult)
                        ins.then_inc(diagonal, 1)
                    if last:
                        pool.wait_ge(valued, (h + 1) * TILES + 1)
                        load_values(g + 1, 1)

                load_values(0, 0)
                load_values(0, 1)
                heads(pool, head)
                for half in range(2):
                    pool.wait_ge(v_loaded[half], (KVB + 1) * 32)

            @block.tensor
            def _(pe):
                def row(g, h, i, r):
                    if r == 0:
                        pe.wait_ge(q_low, h * NC + i + 2)
                        pe.wait_ge(k_low, g * NC + i + 2)
                    before = h * NT + i * TPC
                    if i == 0:
                        if not isinstance(h, int):
                            pe.wait_ge(exped, before + 1)
                    elif i == 1:
                        pe.wait_ge(exped, (before - TPC + 2 * r + 2 if r < 2 else before + r - 1) + 1)
                    else:
                        pe.wait_ge(exped, before + r + 1)
                    b0 = r * CH if i == 0 else (r % 2) * 2 * CH if i == 1 else 0
                    for c in range(i + 1):
                        w = CH if c < i else (r + 1) * P
                        wide = max(w, 2 * P)
                        out = ps[:, b0 + c * CH:b0 + c * CH + wide]
                        last = three_products(nc, out, q_hi[:, i % 2, r * P:(r + 1) * P],
                                              q_lo[:, i % 2, r * P:(r + 1) * P],
                                              k_hi[:, c * CH:c * CH + wide], k_lo[:, c * CH:c * CH + wide],
                                              True, c < i)
                        if c == i:
                            e = b0 + c * CH + w
                            last = nc.tensor.matmul(ps[:, e - P:e], core.identb[:], core.maskq[:],
                                                    start=False, stop=True, skip_group_check=True)
                        if c == i or (i >= 2 and c == 1):
                            last.then_inc(scored, 1)

                def head(g, h, last):
                    def turn(i, kt):
                        n = slot0[i] + kt
                        if kt == 0:
                            pe.wait_ge(exped, h * NT + (i + 1) * TPC + 1)
                        if n < 3:
                            pe.wait_ge(spread_out, h * NC + 1)
                        elif kt < 3:
                            pe.wait_ge(spread_out, h * NC + i + 1)
                        g = max(0, kt - i * TPC)
                        for r in range(g, TPC):
                            last = nc.tensor.transpose(pt[:, n % 3, r * P:(r + 1) * P],
                                                       p[:, i % 2, r, kt * P:(kt + 1) * P], core.ident[:])
                        last.then_inc(turned, 1)

                    def product(i, kt):
                        n = tiles0[i] + kt
                        m = max(0, kt - i * TPC)
                        pe.wait_ge(low, h * TILES + n + 2)
                        pe.wait_ge(high, h * TILES + n + 2)
                        if kt == NT // 2 * (i // 2) and i in (0, 2):
                            pe.wait_ge(v_loaded[i // 2], (g + 1) * 32)
                        if kt == 0:
                            pe.wait_ge(o_ready, h * NC + i + 1)
                        last = three_products(nc, po[:, m * P:], v_hi[:, kt, :], v_lo[:, kt, :],
                                              pT_hi[:, n % 3, m * P:], pT_lo[:, n % 3, m * P:],
                                              kt == 0, kt == TPC * (i + 1) - 1)
                        last.then_inc(valued, 1)

                    def finish(i):
                        pe.wait_ge(diagonal, h * NC + i + 2)
                        n = slot0[i] + TPC * (i + 1)
                        nc.tensor.matmul(pt[:, n % 3, :], core.ones[:], diag[:].rearrange("p r q -> p (r q)"),
                                         start=True, stop=True, skip_group_check=True).then_inc(spread, 1)

                    for i in range(1, NC + 1):
                        for what, n in beside(i):
                            if what == "row" and i < NC:
                                row(g, h, i, n)
                            elif what == "row":
                                row(g + last, h + 1, 0, n)
                            elif what == "turn":
                                turn(i - 1, n)
                            elif what == "product":
                                product(i - 1, n)
                        finish(i - 1)

                for r in range(TPC):
                    row(0, 0, 0, r)
                heads(pe, head)

            @block.scalar
            def _(act):
                def k_split(g, c):
                    act.wait_ge(k_loaded, (g + 1) * 16 + 1)
                    nc.scalar.activation(k_hi[:, c * CH:(c + 1) * CH], k_raw[:, c * CH:(c + 1) * CH],
                                         ACT.Copy).then_inc(k_high, 1)

                def q_split(h, i):
                    act.wait_ge(q_loaded[i % 2], h * (NC // 2 * 16) + (i // 2 + 1) * 16 + 1)
                    if i >= 1:
                        act.wait_ge(scored, h * PARTS + part0[i - 1] + 1)
                    elif not isinstance(h, int):
                        act.wait_ge(scored, h * PARTS - TPC * parts[NC - 1] + 1)
                    nc.scalar.activation(q_hi[:, i % 2, :], q_raw[:, i % 2, :], ACT.Copy).then_inc(q_high, 1)

                def exp_row(h, i, r):
                    act.wait_ge(biased, h * NT + i * TPC + r + 2)
                    if i >= 1:
                        act.wait_ge(turned, h * TILES + tiles0[i - 1] + 1)
                        act.wait_ge(inverted, h * NC + i)
                    elif not isinstance(h, int):
                        act.wait_ge(turned, h * TILES - TPC * NC + 1)
                        act.wait_ge(inverted, h * NC)
                    b0 = r * CH if i == 0 else (r % 2) * 2 * CH if i == 1 else 0
                    w = (i * TPC + r + 1) * P
                    nc.scalar.activation(p[:, i % 2, r, 0:w], ps[:, b0:b0 + w], ACT.Exp,
                                         bias=bias[:, i % 2, r:r + 1], scale=SCALE_B,
                                         accum_out=rsum[:, i % 2, r:r + 1]).then_inc(exped, 1)

                def head(g, h, last):
                    def high_part(i, kt):
                        n = tiles0[i] + kt
                        m = max(0, kt - i * TPC)
                        act.wait_ge(turned, h * TILES + n + 2)
                        act.wait_ge(valued, h * TILES + max(0, n - 2) + 1)
                        nc.scalar.activation(pT_hi[:, n % 3, m * P:], pt[:, (slot0[i] + kt) % 3, m * P:],
                                             ACT.Copy).then_inc(high, 1)

                    def spread_copy(i):
                        act.wait_ge(spread, h * NC + i + 2)
                        act.wait_ge(o_ready, h * NC + i + 1)
                        nc.scalar.activation(r_sb[:], pt[:, (slot0[i] + TPC * (i + 1)) % 3, :],
                                             ACT.Copy).then_inc(spread_out, 1)

                    def store(i):
                        act.wait_ge(o_ready, h * NC + i + 2)
                        dst = core.o_b[:, bass.ds(h, 1), i * CH:(i + 1) * CH].rearrange("p a t -> p (a t)")
                        act.dma_start(dst, o_sb[:, i % 2, :]).then_inc(o_stored[i % 2], 16)

                    for i in range(1, NC + 1):
                        if i == NC:
                            q_split(h + 1, 0)
                        for what, n in beside(i):
                            if what == "row":
                                if i < NC:
                                    exp_row(h, i, n)
                                else:
                                    exp_row(h + 1, 0, n)
                                if n == 1:
                                    if i == NC:
                                        q_split(h + 1, 1)
                                    elif i + 1 < NC:
                                        q_split(h, i + 1)
                                    if i >= 2:
                                        store(i - 2)
                            elif what == "turn":
                                high_part(i - 1, n)
                            elif what == "keys" and last:
                                if n == 0:
                                    act.wait_ge(scored, (h + 1) * PARTS + 1)
                                k_split(g + 1, n)
                        spread_copy(i - 1)
                    store(NC - 1)

                for c in range(NC):
                    k_split(0, c)
                q_split(0, 0)
                for r in range(TPC):
                    exp_row(0, 0, r)
                q_split(0, 1)
                heads(act, head)

            @block.vector
            def _(dve):
                def k_split(g, c):
                    dve.wait_ge(k_high, g * NC + c + 2)
                    nc.vector.tensor_tensor(k_lo[:, c * CH:(c + 1) * CH], k_raw[:, c * CH:(c + 1) * CH],
                                            k_hi[:, c * CH:(c + 1) * CH], ALU.subtract).then_inc(k_low, 1)

                def q_split(h, i):
                    dve.wait_ge(q_high, h * NC + i + 2)
                    nc.vector.tensor_tensor(q_lo[:, i % 2, :], q_raw[:, i % 2, :], q_hi[:, i % 2, :],
                                            ALU.subtract).then_inc(q_low, 1)

                def max_row(h, i, r):
                    b0 = r * CH if i == 0 else (r % 2) * 2 * CH if i == 1 else 0
                    w = (i * TPC + r + 1) * P
                    s0 = h * PARTS + part0[i] + r * parts[i]
                    cuts = [0, w] if parts[i] == 1 else [0, 2 * CH, w]
                    for k in range(parts[i]):
                        dve.wait_ge(scored, s0 + k + 2)
                        nc.vector.tensor_reduce(mx[:, r, k:k + 1], ps[:, b0 + cuts[k]:b0 + cuts[k + 1]],
                                                axis=AX.X, op=ALU.max, negate=True).then_inc(maxed, 1)
                    dve.wait_ge(maxed, s0 + parts[i] + 1)
                    other = mx[:, r, 1:2] if parts[i] == 2 else mx[:, r, 0:1]
                    nc.vector.tensor_scalar(bias[:, i % 2, r:r + 1], mx[:, r, 0:1], other, SCALE_B,
                                            ALU.min, ALU.mult).then_inc(biased, 1)

                def head(g, h, last):
                    def low_part(i, kt):
                        n = tiles0[i] + kt
                        m = max(0, kt - i * TPC)
                        dve.wait_ge(high, h * TILES + n + 2)
                        nc.vector.tensor_tensor(pT_lo[:, n % 3, m * P:], pt[:, (slot0[i] + kt) % 3, m * P:],
                                                pT_hi[:, n % 3, m * P:], ALU.subtract).then_inc(low, 1)

                    def invert(i):
                        dve.wait_ge(exped, h * NT + (i + 1) * TPC + 1)
                        dve.wait_ge(diagonal, h * NC + i + 1)
                        nc.vector.reciprocal(rrec[:], rsum[:, i % 2, :]).then_inc(inverted, 1)

                    def output(i):
                        dve.wait_ge(spread_out, h * NC + i + 2)
                        dve.wait_ge(o_stored[i % 2], h * (NC // 2 * 16) + (i // 2) * 16 + 1)
                        nc.vector.tensor_tensor(o_sb[:, i % 2, :], po[:], r_sb[:], ALU.mult).then_inc(o_ready, 1)

                    for i in range(1, NC + 1):
                        if i == NC:
                            q_split(h + 1, 0)
                        for what, n in beside(i):
                            if what == "row":
                                if i < NC:
                                    max_row(h, i, n)
                                else:
                                    max_row(h + 1, 0, n)
                                if n == 0:
                                    invert(i - 1)
                                if n == 1:
                                    if i == NC:
                                        q_split(h + 1, 1)
                                    elif i + 1 < NC:
                                        q_split(h, i + 1)
                            elif what == "turn":
                                low_part(i - 1, n)
                            elif what == "keys" and last:
                                k_split(g + 1, n)
                        output(i - 1)

                for c in range(NC):
                    k_split(0, c)
                q_split(0, 0)
                for r in range(TPC):
                    max_row(0, 0, r)
                q_split(0, 1)
                heads(dve, head)


def phase_output_b(core, wob_in):
    nc = core.nc
    with ExitStack() as st:
        sb = phase_sbuf(nc, st)
        wo = sb("wob", [P, HB, D])
        wo_hi = sb("wob_hi", [P, HB, D], F32R)
        wo_lo = sb("wob_lo", [P, HB, D], F32R)
        o_raw = [sb(f"o_raw{i}", [P, HB, P]) for i in range(2)]
        o_hi = [sb(f"o_hi{i}", [P, HB, P], F32R) for i in range(2)]
        o_lo = [sb(f"o_lo{i}", [P, HB, P], F32R) for i in range(2)]
        py = st.enter_context(nc.psum_tensor("py_ob", [P, 2, CH], F32))
        w_high, w_split = core.sem("ob_w_high"), core.sem("ob_w_split")
        loaded = [core.sem(f"ob_loaded{i}") for i in range(2)]
        lo_done, y_done, y_out = ([core.sem(f"ob_{n}{i}") for i in range(2)] for n in ("lo", "y_done", "y_out"))
        hi_done = core.sem("ob_hi")
        PARTS = 2

        def heads(part):
            return slice(part * HB // PARTS, (part + 1) * HB // PARTS)

        w_loaded = [core.sem(f"ob_w_loaded{part}") for part in range(PARTS)]
        with nc.Block() as block:
            @block.sync
            def _(sp):
                core.open_semaphores(sp)
                for part in range(PARTS):
                    sp.dma_start(wo[:, heads(part), :], wob_in[:, heads(part), :]).then_inc(w_loaded[part], 16)
                with sp.Fori(0, NT // 2) as j:
                    for i in range(2):
                        sp.wait_ge(lo_done[i], j + 1)
                        sp.dma_start(o_raw[i][:], core.o_b[:, :, bass.ds((2 * j + i) * P, P)]).then_inc(loaded[i], 16)

            @block.tensor
            def _(pe):
                pe.wait_ge(w_split, PARTS + 1)
                with pe.Fori(0, NT // 2) as j:
                    for i in range(2):
                        pe.wait_ge(lo_done[i], j + 2)
                        pe.wait_ge(y_out[i], j + 1)
                        for h in range(HB):
                            last = three_products(nc, py[:, i, 0:D], o_hi[i][:, h, :], o_lo[i][:, h, :],
                                                  wo_hi[:, h, :], wo_lo[:, h, :], h == 0, h == HB - 1)
                        last.then_inc(y_done[i], 1)

            @block.scalar
            def _(act):
                for part in range(PARTS):
                    act.wait_ge(w_loaded[part], 17)
                    nc.scalar.activation(wo_hi[:, heads(part), :], wo[:, heads(part), :], ACT.Copy).then_inc(w_high, 1)
                with act.Fori(0, NT // 2) as j:
                    for i in range(2):
                        act.wait_ge(loaded[i], j * 16 + 17)
                        act.wait_ge(y_done[i], j + 1)
                        nc.scalar.activation(o_hi[i][:], o_raw[i][:], ACT.Copy).then_inc(hi_done, 1)

            @block.vector
            def _(dve):
                def split(j, i):
                    dve.wait_ge(hi_done, 2 * j + i + 2)
                    dve.wait_ge(y_done[i], j + 1)
                    nc.vector.tensor_tensor(o_lo[i][:], o_raw[i][:], o_hi[i][:], ALU.subtract).then_inc(lo_done[i], 1)

                def add(j, i):
                    dve.wait_ge(y_done[i], j + 2)
                    rt = core.R[:, bass.ds(2 * j + i, 1), :].rearrange("p a d -> p (a d)")
                    nc.vector.tensor_tensor(rt, rt, py[:, i, 0:D], ALU.add).then_inc(y_out[i], 1)

                for part in range(PARTS):
                    dve.wait_ge(w_high, part + 2)
                    nc.vector.tensor_tensor(wo_lo[:, heads(part), :], wo[:, heads(part), :], wo_hi[:, heads(part), :],
                                            ALU.subtract).then_inc(w_split, 1)
                split(0, 0)
                with dve.Fori(0, NT // 2 - 1) as j:
                    split(j, 1)
                    add(j, 0)
                    split(j + 1, 0)
                    add(j, 1)
                j = NT // 2 - 1
                split(j, 1)
                add(j, 0)
                add(j, 1)


def phase_experts(core, hT, gates, w13_in, w2_in):
    nc = core.nc
    hT_hi, hT_lo = hT
    with ExitStack() as st:
        sb = phase_sbuf(nc, st)
        w13 = sb("w13", [P, 2, DK, FF])
        w2 = sb("w2", [P, FT, D])
        w13_hi = sb("w13_hi", [P, 2, DK, FF], F32R)
        w13_lo = sb("w13_lo", [P, 2, DK, FF], F32R)
        w2_hi = sb("w2_hi", [P, FT, D], F32R)
        w2_lo = sb("w2_lo", [P, FT, D], F32R)
        s1 = sb("s1", [P, 2, CH])
        gu = sb("gu", [P, 2, CH])
        g_hi = sb("g_hi", [P, FT, CH], F32R)
        g_lo = sb("g_lo", [P, FT, CH], F32R)
        ph = st.enter_context(nc.psum_tensor("ph_e", [P, 2, 2, CH], F32))
        py = st.enter_context(nc.psum_tensor("py_e", [P, 4, CH], F32))
        w13_loaded, w13_high, w13_low = (core.sem(f"e_w13_{n}") for n in ("loaded", "high", "low"))
        w2_loaded, w2_high, w2_low = (core.sem(f"e_w2_{n}") for n in ("loaded", "high", "low"))
        mixed, silued, gated, g_high, g_low = (core.sem(f"e_{n}") for n in ("mixed", "silued", "gated", "g_high", "g_low"))
        y_parts, y_out = core.sem("e_y_parts"), core.sem("e_y_out")

        def chunks(eng, chunk):
            with eng.Fori(0, NE - 1) as e:
                chunk(e, 0, (e, 1))
                with eng.Fori(1, NC - 1) as c:
                    chunk(e, c, (e, c + 1))
                chunk(e, NC - 1, (e + 1, 0))
            e = NE - 1
            chunk(e, 0, (e, 1))
            with eng.Fori(1, NC - 1) as c:
                chunk(e, c, (e, c + 1))
            chunk(e, NC - 1, None)

        def slice13(w, f):
            return w[:, :, :, f * P:(f + 1) * P]

        with nc.Block() as block:
            @block.sync
            def _(sp):
                core.open_semaphores(sp)
                with sp.Fori(0, NE) as e:
                    sp.wait_ge(w13_low, e * FT + 1)
                    sp.dma_start(w13[:], w13_in[bass.ds(e, 1)].rearrange("a p w k f -> (a p) w k f")).then_inc(w13_loaded, 16)
                    sp.wait_ge(w2_low, e * FT + 1)
                    sp.dma_start(w2[:], w2_in[bass.ds(e, 1)].rearrange("a p f d -> (a p) f d")).then_inc(w2_loaded, 16)

            @block.tensor
            def _(pe):
                def mix(e, c, f):
                    n = e * NC + c
                    pe.wait_ge(w13_low, e * FT + f + 2)
                    pe.wait_ge(gated, (n * FT + f - 1 if f >= 2 else n * FT) + 1)
                    tokens = bass.ds(c * CH, CH)
                    for w in range(2):
                        for dk in range(DK):
                            last = three_products(
                                nc, ph[:, f % 2, w, :], w13_hi[:, w, dk, f * P:(f + 1) * P],
                                w13_lo[:, w, dk, f * P:(f + 1) * P],
                                hT_hi[:, dk, tokens], hT_lo[:, dk, tokens], dk == 0, dk == DK - 1)
                    last.then_inc(mixed, 1)

                def multiply(e, c, f):
                    n = e * NC + c
                    pe.wait_ge(g_low, n * FT + f + 2)
                    pe.wait_ge(w2_low, e * FT + f + 2)
                    if f == 0:
                        pe.wait_ge(y_out, n * TPC + 1)
                    for t in range(TPC):
                        three_products(nc, py[:, t, 0:D], g_hi[:, f, t * P:(t + 1) * P],
                                       g_lo[:, f, t * P:(t + 1) * P], w2_hi[:, f, :], w2_lo[:, f, :],
                                       f == 0, f == FT - 1).then_inc(y_parts, 1)

                def chunk(e, c, following):
                    for f in range(1, FT):
                        mix(e, c, f)
                        multiply(e, c, f - 1)
                    if following is not None:
                        mix(*following, 0)
                    multiply(e, c, FT - 1)
                mix(0, 0, 0)
                chunks(pe, chunk)

            @block.scalar
            def _(act):
                def gate_tile(e, c, f, held):
                    n = e * NC + c
                    act.wait_ge(mixed, n * FT + f + 2)
                    act.wait_ge(gated, (n * FT + f - 1 if f >= 2 else n * FT) + 1)
                    nc.scalar.activation(s1[:, f % 2, :], ph[:, f % 2, 0, :], ACT.Silu).then_inc(silued, 1)
                    act.wait_ge(gated, n * FT + f + 2)
                    act.wait_ge(y_parts, held)
                    nc.scalar.activation(g_hi[:, f, :], gu[:, f % 2, :], ACT.Copy).then_inc(g_high, 1)

                def split13(e, f):
                    if f == 0:
                        act.wait_ge(w13_loaded, e * 16 + 17)
                    if not isinstance(e, int):
                        act.wait_ge(mixed, e * (NC * FT) - FT + f + 2)
                    nc.scalar.activation(slice13(w13_hi, f), slice13(w13, f), ACT.Copy).then_inc(w13_high, 1)

                def split2(e, f):
                    if f == 0:
                        act.wait_ge(w2_loaded, e * 16 + 17)
                        act.wait_ge(y_parts, e * (NC * FT * TPC) + 1)
                    nc.scalar.activation(w2_hi[:, f, :], w2[:, f, :], ACT.Copy).then_inc(w2_high, 1)

                def chunk(e, c, following):
                    n = e * NC + c
                    for f in range(1, FT):
                        if isinstance(c, int) and c == 0:
                            split2(e, f - 1)
                        gate_tile(e, c, f, n * (FT * TPC) + 1)
                        if isinstance(c, int) and c == NC - 1 and following is not None:
                            split13(e + 1, f - 1)
                    if isinstance(c, int) and c == 0:
                        split2(e, FT - 1)
                    if following is not None:
                        gate_tile(*following, 0, n * (FT * TPC) + TPC + 1)
                    if isinstance(c, int) and c == NC - 1 and following is not None:
                        split13(e + 1, FT - 1)
                for f in range(FT):
                    split13(0, f)
                gate_tile(0, 0, 0, 1)
                chunks(act, chunk)

            @block.vector
            def _(dve):
                def gate_tile(e, c, f, held):
                    n = e * NC + c
                    dve.wait_ge(silued, n * FT + f + 2)
                    dve.wait_ge(g_low, (n * FT + f - 1 if f >= 2 else n * FT) + 1)
                    nc.vector.tensor_tensor(gu[:, f % 2, :], s1[:, f % 2, :], ph[:, f % 2, 1, :],
                                            ALU.mult).then_inc(gated, 1)
                    dve.wait_ge(g_high, n * FT + f + 2)
                    dve.wait_ge(y_parts, held)
                    nc.vector.tensor_tensor(g_lo[:, f, :], gu[:, f % 2, :], g_hi[:, f, :],
                                            ALU.subtract).then_inc(g_low, 1)

                def split13(e, f):
                    dve.wait_ge(w13_high, e * FT + f + 2)
                    nc.vector.tensor_tensor(slice13(w13_lo, f), slice13(w13, f), slice13(w13_hi, f),
                                            ALU.subtract).then_inc(w13_low, 1)

                def split2(e, f):
                    dve.wait_ge(w2_high, e * FT + f + 2)
                    nc.vector.tensor_tensor(w2_lo[:, f, :], w2[:, f, :], w2_hi[:, f, :],
                                            ALU.subtract).then_inc(w2_low, 1)

                def output(e, c, t):
                    n = e * NC + c
                    dve.wait_ge(y_parts, n * (FT * TPC) + (FT - 1) * TPC + t + 2)
                    rt = core.R[:, bass.ds(c * TPC + t, 1), :].rearrange("p a d -> p (a d)")
                    gate = gates[:, bass.ds(c * TPC + t, 1), bass.ds(e, 1)].rearrange("p a b -> p (a b)")
                    nc.vector.scalar_tensor_tensor(rt, py[:, t, 0:D], gate, rt, ALU.mult, ALU.add).then_inc(y_out, 1)

                def chunk(e, c, following):
                    n = e * NC + c
                    for f in range(1, FT):
                        if isinstance(c, int) and c == 0:
                            split2(e, f - 1)
                        gate_tile(e, c, f, n * (FT * TPC) + 1)
                        if isinstance(c, int) and c == NC - 1 and following is not None:
                            split13(e + 1, f - 1)
                    if isinstance(c, int) and c == 0:
                        split2(e, FT - 1)
                    if following is not None:
                        gate_tile(*following, 0, n * (FT * TPC) + TPC + 1)
                    for t in range(TPC):
                        output(e, c, t)
                    if isinstance(c, int) and c == NC - 1 and following is not None:
                        split13(e + 1, FT - 1)
                for f in range(FT):
                    split13(0, f)
                gate_tile(0, 0, 0, 1)
                chunks(dve, chunk)


def phase_route(core, gates, tri_in):
    nc = core.nc
    with ExitStack() as st:
        sb = phase_sbuf(nc, st)
        tri = sb("tri", [P, NE, NE])
        gt = sb("gt", [P, NT, NE, NE])
        eq = sb("eq", [P, NT, NE, NE])
        rank = sb("rank", [P, NT, NE])
        top = sb("top", [P, NT, 1])
        ex = sb("ex", [P, NT, NE])
        tot = sb("tot", [P, NT, 1])
        loaded, chained, shifted, exped = (core.sem(f"rt_{n}") for n in ("loaded", "chained", "shifted", "exped"))
        with nc.Block() as block:
            @block.sync
            def _(sp):
                core.open_semaphores(sp)
                sp.dma_start(tri[:], tri_in).then_inc(loaded, 16)

            @block.scalar
            def _(act):
                act.wait_ge(shifted, 2)
                nc.scalar.activation(ex[:], gates[:], ACT.Exp).then_inc(exped, 1)

            @block.vector
            def _(dve):
                chain = Chain(dve, chained, core.passed)
                dve.wait_ge(loaded, 17)
                lg = core.logits
                chain.link(nc.vector.tensor_reduce(top[:], lg[:], axis=AX.X, op=ALU.max))
                nc.vector.tensor_tensor(gates[:], lg[:], top[:].broadcast_to([P, NT, NE]), ALU.subtract).then_inc(shifted, 1)
                for t in range(NT):
                    lj = lg[:, t:t + 1, :].broadcast_to([P, NE, NE])
                    le = lg[:, t, :].rearrange("p (e a) -> p e a", a=1).broadcast_to([P, NE, NE])
                    nc.vector.tensor_tensor(gt[:, t, :, :], lj, le, ALU.is_gt)
                    last = nc.vector.tensor_tensor(eq[:, t, :, :], lj, le, ALU.is_equal)
                chain.link(last)
                for t in range(NT):
                    last = nc.vector.tensor_tensor(eq[:, t, :, :], eq[:, t, :, :], tri[:], ALU.mult)
                chain.link(last)
                chain.link(nc.vector.tensor_tensor(gt[:], gt[:], eq[:], ALU.add))
                chain.link(nc.vector.tensor_reduce(rank[:], gt[:], axis=AX.X, op=ALU.add))
                chain.link(nc.vector.tensor_scalar(rank[:], rank[:], float(TOPK) - 0.5, None, ALU.is_lt))
                dve.wait_ge(exped, 2)
                chain.link(nc.vector.tensor_tensor(ex[:], ex[:], rank[:], ALU.mult))
                chain.link(nc.vector.tensor_reduce(tot[:], ex[:], axis=AX.X, op=ALU.add))
                chain.link(nc.vector.reciprocal(tot[:], tot[:]))
                chain.link(nc.vector.tensor_tensor(gates[:], ex[:], tot[:].broadcast_to([P, NT, NE]), ALU.mult))


def phase_final(core, out):
    nc = core.nc
    with ExitStack() as st:
        sb = phase_sbuf(nc, st)
        yn = sb("yn_f", [P, TPC, D])
        rooted, stored, chained = core.sem("f_rooted"), core.sem("f_stored"), core.sem("f_chained")
        with nc.Block() as block:
            @block.scalar
            def _(act):
                for c in range(NC):
                    root(core, act, core.rstd[:], core.mv[:, :, 1:2], chained, 5 * c + 2, rooted)

            @block.vector
            def _(dve):
                for c in range(NC):
                    chain = Chain(dve, chained, core.passed, 5 * c)
                    layer_norm_stats(nc, chain, core, lambda t: core.R[:, c * TPC + t, :], rooted, c + 1)
                    for t in range(TPC):
                        last = nc.vector.tensor_scalar(yn[:, t, :], core.R[:, c * TPC + t, :], core.mv[:, t, 0:1],
                                                       core.rstd[:, t, :], ALU.subtract, ALU.mult)
                    chain.link(last)
                    Xc = core.X[:, c * TPC:(c + 1) * TPC, :]
                    ins = nc.vector.tensor_tensor(Xc, Xc, yn[:], ALU.add)
                    chain.link(ins)

            @block.sync
            def _(sp):
                core.open_semaphores(sp)
                for c in range(NC):
                    sp.wait_ge(chained, 5 * (c + 1) + 1)
                    sp.dma_start(out[:, c * TPC:(c + 1) * TPC, :], core.X[:, c * TPC:(c + 1) * TPC, :]).then_inc(stored, 16)
                sp.wait_ge(stored, NC * 16 + 1)


def program(nc, x, ident, identb, maskq, maskt, wcol, cos_a, sin_a, cos_b, sin_b, wa, woa, wqkv, wob,
            gate, tri, w13, w2, out, stop=99, dbg=None):
    with ExitStack() as root:
        core = Core(nc, root)
        core.qk_a = core.scratch("qk_a", [2 * HA, 2, HDA, T])
        core.q_b = core.scratch("q_b", [HB + 1, P, T])
        core.k_b = core.scratch("k_b", [KVB + 1, P, T])
        core.v_b = core.scratch("v_b", [KVB + 1, 2, P, NT, HDB])
        core.o_b = core.scratch("o_b", [P, HB, T])
        core.X = core.keep("X", [P, NT, D])
        core.R = core.keep("R", [P, NT, D])
        core.ident = core.keep("ident", [P, P])
        core.identb = core.keep("identb", [P, P], BF16)
        core.ones = core.keep("ones", [P, P])
        core.eps = core.keep("eps", [P, 1])
        core.maskq = core.keep("maskq", [P, P], BF16)
        core.maskt = core.keep("maskt", [P, 3 * P + CH], BF16)
        core.wcol = core.keep("wcol", [P, 3, DK])
        core.stats = core.keep("stats", [P, TPC, 6])
        core.mv = core.keep("mv", [P, TPC, 2])
        core.rstd = core.keep("rstd", [P, TPC, 1])
        core.logits = core.keep("logits", [P, NT, NE])
        gates = core.keep("gates", [P, NT, NE])
        gate_w = core.keep("gate_w", [P, DK, NE])

        def load(sp, loaded):
            for dst, src in ((core.X, x), (core.ident, ident), (core.identb, identb), (core.maskq, maskq),
                             (core.maskt, maskt), (core.wcol, wcol), (gate_w, gate)):
                sp.dma_start(dst[:], src).then_inc(loaded, 16)
        load.count = 7

        def hT_buffers(stack, tag):
            sb = phase_sbuf(nc, stack)
            return sb(f"hT_hi_{tag}", [P, DK, T], F32R), sb(f"hT_lo_{tag}", [P, DK, T], F32R)

        with ExitStack() as st:
            sb = phase_sbuf(nc, st)
            V_all = sb("V_all", [P, NT, D])
            O_all = sb("O_all", [P, NT, D])
            with ExitStack() as st1:
                hT = hT_buffers(st1, "a")
                phase_norm(core, "a", "ln", hT, load=load)
                phase_project_a(core, hT, V_all, wa, cos_a, sin_a)
            phase_attention_a(core, V_all, O_all)
            phase_output_a(core, O_all, woa)
        with ExitStack() as st:
            hT = hT_buffers(st, "b")
            phase_norm(core, "b", "ln_rms", hT)
            phase_project_b(core, hT, wqkv, None, cos_b, sin_b)
        phase_attention_b(core)
        phase_output_b(core, wob)
        with ExitStack() as st:
            hT = hT_buffers(st, "m")
            phase_norm(core, "m", "rms", hT, gate=gate_w)
            phase_route(core, gates, tri)
            phase_experts(core, hT, gates, w13, w2)
        phase_final(core, out)


def shape_constants():
    f = np.float32
    pos = np.arange(T, dtype=f)
    half = HDA // 2
    inv_a = (f(1.0) / np.power(f(10000.0), np.arange(0, HDA, 2, dtype=f) / f(HDA))).astype(f)
    ang_a = (pos[None, :] * inv_a[:, None]).astype(f)
    cos_a = np.tile(np.cos(ang_a).astype(f), (2 * HPT, 1))
    sin_a = np.tile(np.concatenate([-np.sin(ang_a), np.sin(ang_a)]).astype(f), (HPT, 1))
    inv_b = np.power(f(1000000.0), -np.arange(0, HDB, 2, dtype=f) / f(HDB)).astype(f)
    ang_b = (pos[None, :] * inv_b[:, None]).astype(f)
    cos_b = np.concatenate([np.cos(ang_b)] * 2).astype(f)
    sin_b = np.concatenate([-np.sin(ang_b), np.sin(ang_b)]).astype(f)
    bf = mybir.dt.np(BF16)
    i = np.arange(P)
    maskq = np.where(i[None, :] > i[:, None], NEG, 0.0).astype(bf)
    c = np.arange(3 * P + CH) - 3 * P
    maskt = np.where(c[None, :] < i[:, None], NEG, 0.0).astype(bf)
    e = np.arange(NE)
    tri = np.broadcast_to((e[None, :] < e[:, None]).astype(f), (P, NE, NE))
    return dict(ident=np.eye(P, dtype=f), identb=np.eye(P, dtype=f).astype(bf), maskq=maskq, maskt=maskt,
                cos_a=cos_a, sin_a=sin_a, cos_b=cos_b, sin_b=sin_b, tri=np.ascontiguousarray(tri))


def layouts(i):
    def rows(w):
        w = np.asarray(w)
        return np.ascontiguousarray(w.reshape(-1, P, w.shape[-1]).transpose(1, 0, 2))

    wqkv = np.asarray(i["L0_attn_w_qkv"])
    qk = wqkv[:, :2 * D].reshape(D, 2 * HA, 2, HDA // 2)
    swapped = qk[:, :, ::-1, :].reshape(D, 2 * D)

    def pairs(w, n):
        return np.asarray(w).reshape(D, n, HDB // 2, 2).transpose(0, 1, 3, 2).reshape(D, n * HDB)

    wb = np.concatenate([pairs(i["L0_ffn_wq"], HB), pairs(i["L0_ffn_wk"], KVB), np.asarray(i["L0_ffn_wv"])], axis=1)
    w1, w3, w2 = (np.asarray(i[f"L0_ffn_{n}"]) for n in ("w1", "w3", "w2"))
    w13 = np.stack([w1, w3], axis=1).reshape(NE, 2, DK, P, FF).transpose(0, 3, 1, 2, 4)
    ones = np.ones((D,), np.float32)
    wcol = np.stack([ones, np.asarray(i["L0_ffn_ln_w"]), np.asarray(i["L0_ffn_ff_ln_w"])])
    return dict(
        x=rows(np.asarray(i["L0_attn_x"])[0]),
        wcol=np.ascontiguousarray(wcol.reshape(3, DK, P).transpose(2, 0, 1)),
        wa=rows(np.concatenate([wqkv, swapped], axis=1)),
        woa=rows(i["L0_attn_w_o"]),
        wqkv=np.ascontiguousarray(rows(wb).reshape(P, DK, HB + 2 * KVB, HDB)),
        wob=rows(i["L0_ffn_wo"]),
        gate=rows(i["L0_ffn_gate_w"]),
        w13=np.ascontiguousarray(w13),
        w2=np.ascontiguousarray(w2.reshape(NE, FT, P, D).transpose(0, 2, 1, 3)),
    )


def kernel(**inputs):
    import concourse.bacc as bacc
    from concourse.bass_utils import run_bass_kernel_spmd

    nc = bacc.Bacc("TRN2", target_bir_lowering=False, num_devices=1)
    arrays = {**layouts(inputs), **shape_constants()}
    args = {n: nc.dram_tensor(f"in_{n}", a.shape, mybir.dt.from_np(a.dtype), kind="ExternalInput").ap()
            for n, a in arrays.items()}
    out = nc.dram_tensor("out", [P, NT, D], F32, kind="ExternalOutput").ap()
    program(nc, out=out, **args)
    r = run_bass_kernel_spmd(nc, [{f"in_{n}": a for n, a in arrays.items()}], core_ids=[0])
    y = np.asarray(r.results[0]["out"])
    return y.transpose(1, 0, 2).reshape(1, T, D)
```
